# Optimizing a Trainium2 kernel written in Bass

```python
import numpy as np
import jax
import jax.numpy as jnp

def _softmax(x, axis=-1):
    return jax.nn.softmax(x, axis=axis)

def _gelu(x):
    return jax.nn.gelu(x, approximate=True)

def _silu(x):
    return jax.nn.silu(x)

def _sigmoid(x):
    return jax.nn.sigmoid(x)

def _layernorm(x, axis=-1, eps=1e-05):
    m = jnp.mean(x, axis=axis, keepdims=True)
    v = jnp.var(x, axis=axis, keepdims=True)
    return (x - m) / jnp.sqrt(v + eps)

def _scatter_add(tgt, idx, src, axis=0):
    return tgt.at[idx].add(src)

def _segment_sum(src, seg, n):
    return jax.ops.segment_sum(src, seg, n)
kernel_name = 'mk_seq_preln_d1_jaxref_r4_9c2d89'

def setup_inputs(seed: int=0):
    np.random.seed(seed)
    _w = jnp.asarray

    def _L0_attn_setup():
        import jax, jax.numpy as jnp
        import numpy as np
        EMBED_DIM = 256
        NUM_HEADS = 16
        HEAD_DIM = EMBED_DIM // NUM_HEADS
        R_QKV = 64
        R_OUT = 64
        B, T = (4, 512)
        key = jax.random.key(seed)
        k1, k2, k3, k4, k5 = jax.random.split(key, 5)
        s = 0.02
        return {'x': jax.random.normal(k1, (B, T, EMBED_DIM), dtype=jnp.float32), 'W_qkv_v': jax.random.normal(k2, (R_QKV, EMBED_DIM), dtype=jnp.float32) * s, 'W_qkv_u': jax.random.normal(k3, (3 * EMBED_DIM, R_QKV), dtype=jnp.float32) * s, 'W_o_v': jax.random.normal(k4, (R_OUT, EMBED_DIM), dtype=jnp.float32) * s, 'W_o_u': jax.random.normal(k5, (EMBED_DIM, R_OUT), dtype=jnp.float32) * s}
    _L0_attn_in = _L0_attn_setup()

    def _L0_ffn_setup():
        import jax, jax.numpy as jnp
        import numpy as np
        BS, SLEN, DIM = (1, 512, 256)
        NUM_EXPERTS, TOP_K = (8, 2)
        HID = 352

        def _masked_grouped_mm(x, w, onehot):
            g = jnp.einsum('tk,gnk->tgn', x, w, preferred_element_type=jnp.float32)
            return jnp.einsum('tgn,tg->tn', g, onehot)

        def moe_forward(x, gate_w, expert_bias, w_up, w_down, shared_w_up, shared_w_down):
            bs, slen, dim = x.shape
            xf = x.reshape(-1, dim)
            scores = jax.nn.sigmoid((xf @ gate_w.T).astype(jnp.float32))
            biased = scores + expert_bias
            _, sel = jax.lax.top_k(biased, TOP_K)
            top_scores = jnp.take_along_axis(scores, sel, axis=-1)
            flat_sel = sel.reshape(-1)
            counts = jnp.bincount(flat_sel, length=NUM_EXPERTS)
            order = jnp.argsort(flat_sel, stable=True)
            scores_sorted = top_scores.reshape(-1)[order]
            token_ids = order // TOP_K
            routed_in = (xf[token_ids] * scores_sorted[:, None]).astype(x.dtype)
            seg = jnp.repeat(jnp.arange(NUM_EXPERTS), counts, total_repeat_length=flat_sel.shape[0])
            onehot = jax.nn.one_hot(seg, NUM_EXPERTS, dtype=jnp.float32)
            h = _masked_grouped_mm(routed_in.astype(jnp.bfloat16), w_up.astype(jnp.bfloat16), onehot)
            h = jnp.square(jax.nn.relu(h.astype(jnp.bfloat16)))
            routed_out = _masked_grouped_mm(h.astype(jnp.bfloat16), w_down.astype(jnp.bfloat16), onehot)
            routed_out = routed_out.astype(jnp.bfloat16).astype(x.dtype)
            hs = jnp.square(jax.nn.relu(xf @ shared_w_up.T))
            shared_out = hs @ shared_w_down.T
            combined = jnp.zeros((flat_sel.shape[0], dim), routed_out.dtype).at[order].set(routed_out)
            out = combined.reshape(-1, TOP_K, dim).sum(axis=1) + shared_out
            return out.reshape(bs, slen, dim)
        key = jax.random.key(seed)
        k = jax.random.split(key, 6)
        s = 0.02
        return {'x': jax.random.normal(k[0], (BS, SLEN, DIM), jnp.float32), 'gate_w': jax.random.normal(k[1], (NUM_EXPERTS, DIM), jnp.float32) * s, 'expert_bias': jnp.zeros((NUM_EXPERTS,), jnp.float32), 'w_up': jax.random.normal(k[2], (NUM_EXPERTS, HID, DIM), jnp.float32) * s, 'w_down': jax.random.normal(k[3], (NUM_EXPERTS, DIM, HID), jnp.float32) * s, 'shared_w_up': jax.random.normal(k[4], (HID, DIM), jnp.float32) * s, 'shared_w_down': jax.random.normal(k[5], (DIM, HID), jnp.float32) * s}
    _L0_ffn_in = _L0_ffn_setup()
    _d = {'L0_attn_x': _L0_attn_in['x'], 'L0_attn_W_qkv_v': _L0_attn_in['W_qkv_v'], 'L0_attn_W_qkv_u': _L0_attn_in['W_qkv_u'], 'L0_attn_W_o_v': _L0_attn_in['W_o_v'], 'L0_attn_W_o_u': _L0_attn_in['W_o_u'], 'L0_ffn_gate_w': _L0_ffn_in['gate_w'], 'L0_ffn_expert_bias': _L0_ffn_in['expert_bias'], 'L0_ffn_w_up': _L0_ffn_in['w_up'], 'L0_ffn_w_down': _L0_ffn_in['w_down'], 'L0_ffn_shared_w_up': _L0_ffn_in['shared_w_up'], 'L0_ffn_shared_w_down': _L0_ffn_in['shared_w_down']}
    _x0 = _d['L0_attn_x']
    _d['L0_attn_x'] = jax.random.normal(jax.random.fold_in(jax.random.key(seed), 1), (2, 2048, 256), dtype=_x0.dtype)
    del _x0
    return _d

def reference(L0_attn_x, L0_attn_W_qkv_v, L0_attn_W_qkv_u, L0_attn_W_o_v, L0_attn_W_o_u, L0_ffn_gate_w, L0_ffn_expert_bias, L0_ffn_w_up, L0_ffn_w_down, L0_ffn_shared_w_up, L0_ffn_shared_w_down):

    def _L0_attn_ref(x, W_qkv_v, W_qkv_u, W_o_v, W_o_u):
        import jax, jax.numpy as jnp
        import numpy as np
        EMBED_DIM = 256
        NUM_HEADS = 16
        HEAD_DIM = EMBED_DIM // NUM_HEADS
        R_QKV = 64
        R_OUT = 64
        B, T = (4, 512)
        Bq, Tq, C = x.shape
        H, D = (NUM_HEADS, HEAD_DIM)
        qkv = x @ W_qkv_v.T @ W_qkv_u.T
        q, k, v = jnp.split(qkv, 3, axis=-1)
        q = q.reshape(Bq, Tq, H, D).transpose(0, 2, 1, 3)
        k = k.reshape(Bq, Tq, H, D).transpose(0, 2, 1, 3)
        v = v.reshape(Bq, Tq, H, D).transpose(0, 2, 1, 3)
        scale = 1.0 / jnp.sqrt(jnp.asarray(D, dtype=x.dtype))
        scores = jnp.einsum('bhtd,bhsd->bhts', q, k) * scale
        attn = jax.nn.softmax(scores.astype(jnp.float32), axis=-1).astype(q.dtype)
        y = jnp.einsum('bhts,bhsd->bhtd', attn, v)
        y = y.transpose(0, 2, 1, 3).reshape(Bq, Tq, C)
        y = y @ W_o_v.T @ W_o_u.T
        return y

    def _L0_ffn_ref(x, gate_w, expert_bias, w_up, w_down, shared_w_up, shared_w_down):
        import jax, jax.numpy as jnp
        import numpy as np
        BS, SLEN, DIM = (1, 512, 256)
        NUM_EXPERTS, TOP_K = (8, 2)
        HID = 352

        def _masked_grouped_mm(x, w, onehot):
            g = jnp.einsum('tk,gnk->tgn', x, w, preferred_element_type=jnp.float32)
            return jnp.einsum('tgn,tg->tn', g, onehot)

        def moe_forward(x, gate_w, expert_bias, w_up, w_down, shared_w_up, shared_w_down):
            bs, slen, dim = x.shape
            xf = x.reshape(-1, dim)
            scores = jax.nn.sigmoid((xf @ gate_w.T).astype(jnp.float32))
            biased = scores + expert_bias
            _, sel = jax.lax.top_k(biased, TOP_K)
            top_scores = jnp.take_along_axis(scores, sel, axis=-1)
            flat_sel = sel.reshape(-1)
            counts = jnp.bincount(flat_sel, length=NUM_EXPERTS)
            order = jnp.argsort(flat_sel, stable=True)
            scores_sorted = top_scores.reshape(-1)[order]
            token_ids = order // TOP_K
            routed_in = (xf[token_ids] * scores_sorted[:, None]).astype(x.dtype)
            seg = jnp.repeat(jnp.arange(NUM_EXPERTS), counts, total_repeat_length=flat_sel.shape[0])
            onehot = jax.nn.one_hot(seg, NUM_EXPERTS, dtype=jnp.float32)
            h = _masked_grouped_mm(routed_in.astype(jnp.bfloat16), w_up.astype(jnp.bfloat16), onehot)
            h = jnp.square(jax.nn.relu(h.astype(jnp.bfloat16)))
            routed_out = _masked_grouped_mm(h.astype(jnp.bfloat16), w_down.astype(jnp.bfloat16), onehot)
            routed_out = routed_out.astype(jnp.bfloat16).astype(x.dtype)
            hs = jnp.square(jax.nn.relu(xf @ shared_w_up.T))
            shared_out = hs @ shared_w_down.T
            combined = jnp.zeros((flat_sel.shape[0], dim), routed_out.dtype).at[order].set(routed_out)
            out = combined.reshape(-1, TOP_K, dim).sum(axis=1) + shared_out
            return out.reshape(bs, slen, dim)
        return moe_forward(x, gate_w, expert_bias, w_up, w_down, shared_w_up, shared_w_down)
    x = L0_attn_x
    x = x + _L0_attn_ref(_layernorm(x, axis=-1), L0_attn_W_qkv_v, L0_attn_W_qkv_u, L0_attn_W_o_v, L0_attn_W_o_u)
    x = x + _L0_ffn_ref(_layernorm(x, axis=-1), L0_ffn_gate_w, L0_ffn_expert_bias, L0_ffn_w_up, L0_ffn_w_down, L0_ffn_shared_w_up, L0_ffn_shared_w_down)
    return x

_drawn_inputs = setup_inputs


def setup_inputs(seed=0):
    import zlib

    import numpy as np

    out = dict(_drawn_inputs(seed))
    spreads = {'L0_ffn_expert_bias': (0.0, 1.1)}
    factors = {'L0_attn_W_qkv_v': 8.0,
     'L0_attn_W_qkv_u': 8.0,
     'L0_attn_W_o_v': 8.0,
     'L0_attn_W_o_u': 8.0,
     'L0_ffn_gate_w': 10.157,
     'L0_ffn_w_up': 2.927,
     'L0_ffn_w_down': 2.691,
     'L0_ffn_shared_w_up': 8.0,
     'L0_ffn_shared_w_down': 8.0}
    for name, (base, spread) in spreads.items():
        noise = np.random.default_rng([zlib.crc32(name.encode()), seed]).standard_normal(out[name].shape)
        drawn = base * np.exp(spread * noise) if base else spread * noise
        out[name] = jnp.asarray(drawn.astype(out[name].dtype))
    for name, factor in factors.items():
        out[name] = (out[name] * factor).astype(out[name].dtype)
    return out
```

```python
from contextlib import ExitStack

import concourse.bass as bass
from concourse import mybir

P = 128
B, T, C = 2, 2048, 256
NH, HD = 16, 16
RANK = 64
E, HID = 8, 352
EPS = 1e-5
SCALE = HD ** -0.5

CH = 512
TPC = CH // P
KT = C // P
NCHUNK = B * T // CH
HG = 4
NG = B * NH // HG
QPG = T // CH
UNITS = NG * QPG
ST = T // P
NPROD = 6
KROWS = NPROD * HD
QPART = (0, 0, 0, 1, 1, 2)
KPART = (0, 1, 2, 0, 1, 0)
ROWS = KROWS + 3
VW = HD + 1
HT = [P, P, HID - 2 * P]
NHT = len(HT)
SLOTS = E + 1

ALU = mybir.AluOpType
ACT = mybir.ActivationFunctionType
AX = mybir.AxisListType
F32 = mybir.dt.float32
BF16 = mybir.dt.bfloat16


def wait_from_one(eng, sem, value):
    if not isinstance(value, int) or value > 0:
        eng.wait_ge(sem, value)


def wait_alone(eng, sem, value, passed):
    eng.wait_ge(sem, value)
    if not isinstance(value, int):
        eng.sem_inc(passed, 1)


def build(nc, x, wv_t, wu_t, wov_t, wou_t, gate_t, bias_b, wup_t, wdn_t, swup_t, swdn_t,
          ident, tri, sel, out):
    parts_d = nc.dram_tensor("parts_d", [3, 2 * C, B * T], BF16).ap()
    v_d = nc.dram_tensor("v_d", [NG, P, ST, HG * VW], F32).ap()
    x_ch = x.rearrange("b (c t p) d -> (b c) p t d", p=P, t=TPC)
    out_ch = out.rearrange("b (c t p) d -> (b c) p t d", p=P, t=TPC)

    with ExitStack() as ctx:
        psum = ctx.enter_context(nc.psum_tensor("psum", [P, 8, CH], F32))
        identf = ctx.enter_context(nc.sbuf_tensor("identf", [P, P], F32))
        identb = ctx.enter_context(nc.sbuf_tensor("identb", [P, P], BF16))
        y_all = ctx.enter_context(nc.sbuf_tensor("y_all", [P, B * T // P, C], F32))
        project_qkv(nc, psum, identf, identb, x_ch, wv_t, wu_t, ident, parts_d, v_d)
        attend(nc, psum, identf, identb, y_all, parts_d, v_d)
        mix_experts(nc, psum, identf, identb, y_all, x_ch, out_ch, wov_t, wou_t, gate_t, bias_b,
                    wup_t, wdn_t, swup_t, swdn_t, tri, sel)


def project_qkv(nc, psum, identf, identb, x_ch, wv_t, wu_t, ident, parts_d, v_d):
    with ExitStack() as ctx:
        def sb(name, shape, dt=F32):
            return ctx.enter_context(nc.sbuf_tensor(name, shape, dt))

        def sem(name):
            return ctx.enter_context(nc.semaphore(name))

        wv = sb("wv", [P, KT, RANK])
        wu = sb("wu", [RANK, 3 * C])
        xin = sb("xin", [P, 2, TPC, C])
        stats = sb("stats", [P, TPC, 6])
        mv = sb("mv", [P, TPC, 2])
        eps = sb("eps", [P, 1])
        std = sb("std", [P, TPC])
        rstd = sb("rstd", [P, TPC])
        xn = sb("xn", [P, 2, TPC, C])
        xnt = sb("xnt", [P, KT, CH])
        at = sb("at", [RANK, CH])
        parts = sb("parts", [P, 2, 3, 2 * KT, CH], BF16)
        rest = sb("rest", [P, 2 * KT, CH])
        vst = sb("vst", [P, 2, TPC, NH, VW])

        sp_passed = sem("sp_passed")
        dve_passed = sem("dve_passed")
        weights = sem("weights")
        consts = sem("consts")
        x_loaded = [sem("x_loaded0"), sem("x_loaded1")]
        stats_done = sem("stats_done")
        mv_ready = sem("mv_ready")
        std_ready = sem("std_ready")
        rstd_ready = sem("rstd_ready")
        xn_ready = sem("xn_ready")
        xt_psum = sem("xt_psum")
        xt_ready = sem("xt_ready")
        at_psum = sem("at_psum")
        at_ready = sem("at_ready")
        qk_psum = sem("qk_psum")
        v_psum = sem("v_psum")
        part0_ready = sem("part0_ready")
        rest_ready = sem("rest_ready")
        part1_ready = sem("part1_ready")
        part2_ready = sem("part2_ready")
        v_ready = sem("v_ready")
        parts_stored = [sem("parts_stored0"), sem("parts_stored1")]
        v_stored = [sem("v_stored0"), sem("v_stored1")]

        XT, AT, QK, VB = psum[:, 0:2, :], psum[0:RANK, 2, :], psum[:, 3:7, :], (psum[:, 7, :], psum[:, 2, :])
        block = ctx.enter_context(nc.Block())

        @block.sync
        def _(sp):
            def load(i, p):
                sp.dma_start(xin[:, p], x_ch[bass.ds(2 * i + p, 1)].rearrange("o p t d -> p (o t) d")
                             ).then_inc(x_loaded[p], 16)

            def store(i, p):
                n = 2 * i + p
                wait_alone(sp, part2_ready, n + 1, sp_passed)
                for j in range(3):
                    sp.dma_start(parts_d[j, :, bass.ds(n * CH, CH)].rearrange("(m p) t -> p m t", p=P),
                                 parts[:, p, j]).then_inc(parts_stored[p], 16)
                wait_alone(sp, v_ready, n + 1, sp_passed)
                for g in range(NH // HG):
                    group = (n // QPG) * (NH // HG) + g
                    sp.dma_start(v_d[bass.ds(group, 1), :, bass.ds((n % QPG) * TPC, TPC), :]
                                 .rearrange("o p t c -> p (o t) c"),
                                 vst[:, p, :, g * HG:(g + 1) * HG, :].rearrange("p t h c -> p t (h c)")
                                 ).then_inc(v_stored[p], 16)

            load(0, 0)
            sp.dma_start(identf[:], ident).then_inc(weights, 16)
            sp.dma_start(wv[:], wv_t).then_inc(weights, 16)
            sp.dma_start(wu[:], wu_t).then_inc(weights, 16)
            load(0, 1)
            with sp.Fori(0, NCHUNK // 2 - 1) as i:
                for p in range(2):
                    wait_alone(sp, xn_ready, 2 * i + p + 1, sp_passed)
                    load(i + 1, p)
                    store(i, p)
            for p in range(2):
                store(NCHUNK // 2 - 1, p)
            for p in range(2):
                wait_alone(sp, parts_stored[p], 3 * 16 * NCHUNK // 2, sp_passed)
                wait_alone(sp, v_stored[p], (NH // HG) * 16 * NCHUNK // 2, sp_passed)

        @block.vector
        def _(dve):
            def normalise(i, p):
                n = 2 * i + p
                dve.wait_ge(x_loaded[p], 16 * (i + 1))
                wait_from_one(dve, xn_ready, n)
                for t in range(TPC):
                    last = dve.bn_stats(stats[:, t, :], xin[:, p, t, :])
                last.then_inc(stats_done, 1)
                wait_alone(dve, stats_done, n + 1, dve_passed)
                for t in range(TPC):
                    last = dve.bn_aggr(mv[:, t, :], stats[:, t, :])
                last.then_inc(mv_ready, 1)
                dve.wait_ge(std_ready, n + 1)
                dve.reciprocal(rstd[:], std[:]).then_inc(rstd_ready, 1)
                dve.wait_ge(rstd_ready, n + 1)
                wait_from_one(dve, xt_psum, n - 1)
                for t in range(TPC):
                    last = dve.tensor_scalar(xn[:, p, t, :], xin[:, p, t, :], mv[:, t, 0:1],
                                             rstd[:, t:t + 1], ALU.subtract, ALU.mult)
                last.then_inc(xn_ready, 1)

            def take_rest(i, p):
                n = 2 * i + p
                dve.wait_ge(part0_ready, n + 1)
                wait_from_one(dve, part2_ready, n)
                dve.tensor_tensor(rest[:], QK, parts[:, p, 0], ALU.subtract).then_inc(rest_ready, 1)

            dve.memset(eps[:], EPS)
            dve.memset(vst[:, 0, :, :, HD:VW], 1.0)
            dve.memset(vst[:, 1, :, :, HD:VW], 1.0).then_inc(consts, 1)
            dve.wait_ge(weights, 48)
            dve.tensor_copy(identb[:], identf[:]).then_inc(consts, 1)
            normalise(0, 0)
            normalise(0, 1)
            take_rest(0, 0)
            with dve.Fori(1, NCHUNK // 2) as i:
                normalise(i, 0)
                take_rest(i - 1, 1)
                normalise(i, 1)
                take_rest(i, 0)
            take_rest(NCHUNK // 2 - 1, 1)

        @block.gpsimd
        def _(pool):
            def last_part(i, p):
                n = 2 * i + p
                pool.wait_ge(part1_ready, n + 1)
                pool.tensor_tensor(parts[:, p, 2], rest[:], parts[:, p, 1], ALU.subtract
                                   ).then_inc(part2_ready, 1)

            last_part(0, 0)
            with pool.Fori(1, NCHUNK // 2) as i:
                last_part(i - 1, 1)
                last_part(i, 0)
            last_part(NCHUNK // 2 - 1, 1)

        @block.tensor
        def _(pe):
            def transpose_x(i, p):
                n = 2 * i + p
                pe.wait_ge(xn_ready, n + 1)
                wait_from_one(pe, xt_ready, n)
                for k in range(KT):
                    for t in range(TPC):
                        last = pe.transpose(XT[:, k, t * P:(t + 1) * P],
                                            xn[:, p, t, k * P:(k + 1) * P], identf[:])
                last.then_inc(xt_psum, 1)

            def project_down(n):
                pe.wait_ge(xt_ready, n + 1)
                wait_from_one(pe, v_ready, n)
                for k in range(KT):
                    last = pe.matmul(AT, wv[:, k, :], xnt[:, k, :], start=k == 0, stop=k == KT - 1)
                last.then_inc(at_psum, 1)

            def project_up(n):
                pe.wait_ge(at_ready, n + 1)
                wait_from_one(pe, rest_ready, n)
                for m in range(2 * KT):
                    last = pe.matmul(QK[:, m, :], wu[:, m * P:(m + 1) * P], at[:], start=True, stop=True)
                last.then_inc(qk_psum, 1)
                wait_from_one(pe, v_ready, n)
                for t in range(TPC):
                    last = pe.matmul(VB[t // 2][:, (t % 2) * C:(t % 2 + 1) * C], at[:, t * P:(t + 1) * P],
                                     wu[:, 2 * C:3 * C], start=True, stop=True)
                last.then_inc(v_psum, 1)

            pe.wait_ge(weights, 48)
            transpose_x(0, 0)
            with pe.Fori(0, NCHUNK // 2 - 1) as i:
                for p in range(2):
                    project_down(2 * i + p)
                    transpose_x(i + p, 1 - p)
                    project_up(2 * i + p)
            i = NCHUNK // 2 - 1
            project_down(2 * i)
            transpose_x(i, 1)
            project_up(2 * i)
            project_down(2 * i + 1)
            project_up(2 * i + 1)

        @block.scalar
        def _(act):
            def deviation(n):
                act.wait_ge(mv_ready, n + 1)
                act.activation(std[:], mv[:, :, 1], ACT.Sqrt, bias=eps[:]).then_inc(std_ready, 1)

            def copy_xt(n):
                act.wait_ge(xt_psum, n + 1)
                wait_from_one(act, at_psum, n)
                act.activation(xnt[:], XT, ACT.Copy).then_inc(xt_ready, 1)

            def copy_at(n):
                act.wait_ge(at_psum, n + 1)
                wait_from_one(act, v_psum, n)
                act.activation(at[:], AT, ACT.Copy).then_inc(at_ready, 1)

            def copy_qkv(i, p):
                n = 2 * i + p
                act.wait_ge(qk_psum, n + 1)
                wait_from_one(act, parts_stored[p], 48 * i)
                act.activation(parts[:, p, 0], QK, ACT.Copy).then_inc(part0_ready, 1)
                act.wait_ge(v_psum, n + 1)
                wait_from_one(act, v_stored[p], 64 * i)
                for j in range(2):
                    last = act.activation(vst[:, p, 2 * j:2 * j + 2, :, 0:HD],
                                          VB[j].rearrange("p (t h c) -> p t h c", t=2, h=NH), ACT.Copy)
                last.then_inc(v_ready, 1)
                act.wait_ge(rest_ready, n + 1)
                act.activation(parts[:, p, 1], rest[:], ACT.Copy).then_inc(part1_ready, 1)

            act.wait_ge(consts, 1)
            deviation(0)
            copy_xt(0)
            deviation(1)
            with act.Fori(0, NCHUNK // 2 - 1) as i:
                for p in range(2):
                    copy_at(2 * i + p)
                    copy_xt(2 * i + p + 1)
                    copy_qkv(i, p)
                    deviation(2 * i + p + 2)
            i = NCHUNK // 2 - 1
            copy_at(2 * i)
            copy_xt(2 * i + 1)
            copy_qkv(i, 0)
            copy_at(2 * i + 1)
            copy_qkv(i, 1)


def attend(nc, psum, identf, identb, y_all, parts_d, v_d):
    with ExitStack() as ctx:
        def sb(name, shape, dt=F32):
            return ctx.enter_context(nc.sbuf_tensor(name, shape, dt))

        def sem(name):
            return ctx.enter_context(nc.semaphore(name))

        RING = 2 * T
        kst = sb("kst", [ROWS, HG, RING], BF16)
        qst = sb("qst", [ROWS, HG, RING], BF16)
        vcur = sb("vcur", [P, ST, HG, VW])
        PS = 4
        probs = sb("probs", [P, PS, HG, CH])
        SC = T // CH
        mx = sb("mx", [P, 2, HG, SC])
        negmax = sb("negmax", [P, 2, HG])
        mrest = sb("mrest", [P, 2, HG])
        mparts = sb("mparts", [P, 2, 3, HG], BF16)
        mrows = sb("mrows", [3 * HG, 2, P], BF16)
        yt = sb("yt", [P, CH])
        rsum = sb("rsum", [P, TPC, HG])

        sp_passed = sem("sp_passed1")
        pool_passed = sem("pool_passed1")
        ones_set = sem("ones_set")
        acc_zero = sem("acc_zero")
        stacks_loaded = sem("stacks_loaded")
        v_loaded = sem("v_loaded")
        qmax_psum = sem("qmax_psum")
        qmax_done = sem("qmax_done")
        negmax_ready = sem("negmax_ready")
        split_done = sem("split_done")
        mparts_ready = sem("mparts_ready")
        mrows_psum = sem("mrows_psum")
        mrows_ready = sem("mrows_ready")
        mrows_placed = sem("mrows_placed")
        scores_ready = sem("scores_ready")
        probs_ready = sem("probs_ready")
        pv_done = sem("pv_done")
        yt_ready = sem("yt_ready")
        y_psum = sem("y_psum")
        rsum_ready = sem("rsum_ready")
        y_done = sem("y_done")

        SB = [psum[:, h, :] for h in range(HG)]
        MB = [psum[:, 4, :], psum[:, 5, :]]
        ACC = psum[:, 6, :]
        TR = psum[:, 7, :]
        TRB = TR.bitcast(BF16)
        STACK_DMAS = 2 * NPROD
        QT = T // P
        NQ = UNITS * TPC

        block = ctx.enter_context(nc.Block())

        @block.sync
        def _(sp):
            def load_stacks(g):
                batch, row = g // (NH // HG), (g % (NH // HG)) * HG * HD
                cols = (g % 2) * T
                for side, stack, part in ((0, qst, QPART), (1, kst, KPART)):
                    for j in range(NPROD):
                        src = parts_d[part[j], bass.ds(side * C + row, HG * HD), bass.ds(batch * T, T)]
                        sp.dma_start(stack[j * HD:(j + 1) * HD, :, bass.ds(cols, T)],
                                     src.rearrange("(h d) t -> d h t", d=HD)
                                     ).then_inc(stacks_loaded, 16)

            def load_v(g, q):
                sp.dma_start(vcur[:, q * 4:(q + 1) * 4].rearrange("p s h c -> p s (h c)"),
                             v_d[bass.ds(g, 1), :, q * 4:(q + 1) * 4].rearrange("o p s c -> p (o s) c")
                             ).then_inc(v_loaded, 16)

            def next_v(g):
                for q in range(4):
                    wait_alone(sp, pv_done, (QPG * g - 1) * ST + 4 * q + 4, sp_passed)
                    wait_alone(sp, v_loaded, 16 * (4 * g + q), sp_passed)
                    load_v(g, q)

            load_stacks(0)
            for q in range(4):
                load_v(0, q)
                sp.wait_ge(v_loaded, 16 * (q + 1))
            sp.wait_ge(stacks_loaded, 16 * STACK_DMAS)
            load_stacks(1)
            with sp.Fori(1, NG - 1) as g:
                next_v(g)
                wait_alone(sp, scores_ready, HG * ST * QPG * g, sp_passed)
                wait_alone(sp, stacks_loaded, 16 * STACK_DMAS * (g + 1), sp_passed)
                load_stacks(g + 1)
            next_v(NG - 1)

        @block.tensor
        def _(pe):
            def score_max(q, h, c):
                m = (q * HG + h) * SC + c
                wait_from_one(pe, qmax_done, m - 1)
                col = (q % (2 * QT)) * P
                kcol = ((q // QT) % 2) * T + c * CH
                pe.matmul(MB[c % 2], qst[0:KROWS, h, bass.ds(col, P)], kst[0:KROWS, h, bass.ds(kcol, CH)],
                          start=True, stop=True).then_inc(qmax_psum, 1)

            def stack_wait(q):
                pe.wait_ge(stacks_loaded, 16 * STACK_DMAS * (q // QT + 1))

            def turn_maxima(q, par, y_before):
                pe.wait_ge(mparts_ready, q + 1)
                wait_from_one(pe, mrows_ready, q)
                wait_from_one(pe, y_done, y_before)
                pe.transpose(TRB[0:3 * HG, 0:P], mparts[:, par].rearrange("p a h -> p (a h)"),
                             identb[:]).then_inc(mrows_psum, 1)

            def score(u, j, h):
                n = (u * ST + j) * HG + h
                wait_from_one(pe, probs_ready, n - HG + 1)
                qcol = (u % (2 * QPG)) * CH
                kcol = ((u // QPG) % 2) * T + j * P
                pe.matmul(SB[h], kst[:, h, bass.ds(kcol, P)], qst[:, h, bass.ds(qcol, CH)],
                          start=True, stop=True).then_inc(scores_ready, 1)

            def weigh(u, j):
                pe.wait_ge(probs_ready, (u * ST + j + 1) * HG)
                if j % 4 == 0:
                    pe.wait_ge(v_loaded, 16 * (4 * (u // QPG) + j // 4 + 1))
                if j == 0:
                    wait_from_one(pe, yt_ready, u)
                for h in range(HG):
                    last = pe.matmul(ACC[32 * h:32 * h + VW, :], vcur[:, j, h, :], probs[:, j % PS, h, :],
                                     start=j == 0, stop=j == ST - 1)
                last.then_inc(pv_done, 1)

            def turn_y(u, maxima_before):
                pe.wait_ge(yt_ready, u + 1)
                pe.wait_ge(mrows_ready, maxima_before)
                wait_from_one(pe, y_done, u)
                for t in range(TPC):
                    last = pe.transpose(TR[:, t * P:(t + 1) * P], yt[:, t * P:(t + 1) * P], identf[:])
                last.then_inc(y_psum, 1)

            def unit(u, first=False, tiles=TPC, last=False):
                for j in range(ST):
                    q = TPC * (u + 1) + 1 + j // 4
                    ahead = j // 4 < tiles
                    if j % 4 == 0 and ahead:
                        stack_wait(q)
                    if j % 4 == 1 and (j // 4 <= tiles) and not last:
                        turn_maxima(q - 1, (j // 4) % 2, u if j > 3 else 0)
                    if j == 3 and not first:
                        turn_y(u - 1, NQ if last else TPC * (u + 1) + 1)
                    if j == ST - 1 and not last:
                        pe.wait_ge(mrows_placed, 16 * TPC * (u + 2))
                    for h in range(HG):
                        if j < ST - 1:
                            score(u, j + 1, h)
                        elif not last:
                            score(u + 1, 0, h)
                        if ahead:
                            score_max(q, j % 4, h)
                    weigh(u, j)

            pe.wait_ge(ones_set, 1)
            stack_wait(0)
            for q in range(TPC + 1):
                for h in range(HG):
                    for c in range(SC):
                        score_max(q, h, c)
                if q > 0:
                    turn_maxima(q - 1, (q - 1) % 2, 0)
            pe.wait_ge(mrows_placed, 16 * TPC)
            for h in range(HG):
                score(0, 0, h)
            pe.wait_ge(acc_zero, 1)
            unit(0, first=True)
            with pe.Fori(1, UNITS - 2) as u:
                unit(u)
            unit(UNITS - 2, tiles=TPC - 1)
            unit(UNITS - 1, tiles=0, last=True)
            turn_y(UNITS - 1, NQ)

        @block.scalar
        def _(act):
            def exponentials(u, j):
                for h in range(HG):
                    n = (u * ST + j) * HG + h
                    act.wait_ge(scores_ready, n + 1)
                    if h == 0:
                        wait_from_one(act, pv_done, u * ST + j - PS + 1)
                    act.activation(probs[:, j % PS, h, :], SB[h], ACT.Exp, scale=SCALE
                                   ).then_inc(probs_ready, 1)

            def copy_sums(u):
                act.wait_ge(pv_done, (u + 1) * ST)
                wait_from_one(act, y_psum, u)
                act.activation(yt[:], ACC, ACT.Copy).then_inc(yt_ready, 1)

            def unit(u, last=False):
                for j in range(ST - 1):
                    exponentials(u, j + 1)
                if not last:
                    exponentials(u + 1, 0)
                copy_sums(u)

            exponentials(0, 0)
            unit(0)
            with act.Fori(1, UNITS - 1) as u:
                unit(u)
            unit(UNITS - 1, last=True)

        @block.vector
        def _(dve):
            def reduce_head(q, par, h):
                for c in range(SC):
                    m = (q * HG + h) * SC + c
                    dve.wait_ge(qmax_psum, m + 1)
                    dve.tensor_reduce(mx[:, par, h, c:c + 1], MB[c % 2], AX.X, ALU.max
                                      ).then_inc(qmax_done, 1)

            def finish_maxima(q, par):
                dve.wait_ge(qmax_done, (q + 1) * HG * SC)
                wait_from_one(dve, mparts_ready, q - 1)
                dve.tensor_reduce(negmax[:, par, :], mx[:, par], AX.X, ALU.max, negate=True
                                  ).then_inc(negmax_ready, 1)

            def copy_maxima(q, par):
                dve.wait_ge(mrows_psum, q + 1)
                wait_from_one(dve, mrows_placed, 16 * (q - 1))
                dve.tensor_copy(mrows[:, par, :], TRB[0:3 * HG, 0:P]).then_inc(mrows_ready, 1)

            def divide(u):
                dve.wait_ge(y_psum, u + 1)
                heads = TR.rearrange("p (t h c) -> p t h c", t=TPC, h=HG)
                dve.reciprocal(rsum[:], heads[:, :, :, HD]).then_inc(rsum_ready, 1)
                dve.wait_ge(rsum_ready, u + 1)
                batch, group, chunk = u // (UNITS // B), (u // QPG) % (NH // HG), u % QPG
                tile = batch * (T // P) + chunk * TPC
                dst = y_all[:, bass.ds(tile, TPC), bass.ds(group * (HG * HD), HG * HD)]
                dve.tensor_tensor(dst.rearrange("p t (h c) -> p t h c", h=HG), heads[:, :, :, 0:HD],
                                  rsum[:].unsqueeze(3).to_broadcast([P, TPC, HG, HD]), ALU.mult
                                  ).then_inc(y_done, 1)

            def unit(u, first=False, tiles=TPC, last=False):
                for j in range(ST):
                    q = TPC * (u + 1) + 1 + j // 4
                    par = (1 + j // 4) % 2
                    if j // 4 < tiles:
                        reduce_head(q, par, j % 4)
                    if j % 4 == 1 and (j // 4 <= tiles) and not last:
                        copy_maxima(q - 1, 1 - par)
                    if j == 3 and not first:
                        divide(u - 1)
                    if j % 4 == 3 and j // 4 < tiles:
                        finish_maxima(q, par)

            dve.memset(ACC, 0.0).then_inc(acc_zero, 1)
            dve.memset(kst[KROWS:ROWS], 1.0).then_inc(ones_set, 1)
            for q in range(TPC + 1):
                for h in range(HG):
                    reduce_head(q, q % 2, h)
                if q > 0:
                    copy_maxima(q - 1, (q - 1) % 2)
                finish_maxima(q, q % 2)
            unit(0, first=True)
            with dve.Fori(1, UNITS - 2) as u:
                unit(u)
            unit(UNITS - 2, tiles=TPC - 1)
            unit(UNITS - 1, tiles=0, last=True)
            divide(UNITS - 1)

        @block.gpsimd
        def _(pool):
            def split(q, par):
                wait_from_one(pool, mrows_psum, q - 1)
                wait_alone(pool, negmax_ready, q + 1, pool_passed)
                pool.tensor_copy(mparts[:, par, 0], negmax[:, par]).then_inc(split_done, 1)
                wait_alone(pool, split_done, 3 * q + 1, pool_passed)
                pool.tensor_tensor(mrest[:, par], negmax[:, par], mparts[:, par, 0], ALU.subtract
                                   ).then_inc(split_done, 1)
                wait_alone(pool, split_done, 3 * q + 2, pool_passed)
                pool.tensor_copy(mparts[:, par, 1], mrest[:, par]).then_inc(split_done, 1)
                wait_alone(pool, split_done, 3 * q + 3, pool_passed)
                pool.tensor_tensor(mparts[:, par, 2], mrest[:, par], mparts[:, par, 1], ALU.subtract
                                   ).then_inc(mparts_ready, 1)
                pool.wait_ge(mrows_ready, q + 1)
                wait_from_one(pool, mrows_placed, 16 * q)
                pool.dma_start(qst[KROWS:ROWS, :, bass.ds((q % (2 * QT)) * P, P)],
                               mrows[:, par, :]
                               ).then_inc(mrows_placed, 16)

            split(0, 0)
            split(1, 1)
            with pool.Fori(1, NQ // 2) as i:
                split(2 * i, 0)
                split(2 * i + 1, 1)
            pool.wait_ge(mrows_placed, 16 * NQ)


def mix_experts(nc, psum, identf, identb, y_all, x_ch, out_ch, wov_t, wou_t, gate_t, bias_b,
                wup_t, wdn_t, swup_t, swdn_t, tri, sel):
    with ExitStack() as ctx:
        def sb(name, shape, dt=F32):
            return ctx.enter_context(nc.sbuf_tensor(name, shape, dt))

        def sem(name):
            return ctx.enter_context(nc.semaphore(name))

        wov = sb("wov", [P, KT, RANK])
        wou = sb("wou", [RANK, C])
        gate = sb("gate", [P, KT, E])
        bias = sb("bias", [P, E])
        lower = sb("lower", [P, E * E])
        pick = sb("pick", [3 * E, E, P], BF16)
        pickf = sb("pickf", [3 * E, E, P])
        wup = sb("wup", [P, E, KT, HID], BF16)
        wdn = sb("wdn", [P, E, NHT, C], BF16)
        swup = sb("swup", [P, KT, HID])
        swdn = sb("swdn", [P, NHT, C])

        yb = sb("yb", [P, 2, TPC, C])
        acc = sb("acc", [P, 2, TPC, C])
        ybt = sb("ybt", [P, KT, CH])
        zt = sb("zt", [RANK, CH])
        stats = sb("stats2", [P, TPC, 6])
        mv = sb("mv2", [P, TPC, 2])
        eps = sb("eps2", [P, 1])
        std = sb("std2", [P, TPC])
        rstd = sb("rstd2", [P, TPC])
        xn = sb("xn2", [P, TPC, C])
        xnt = sb("xnt2", [P, 2, KT, CH])
        neg = sb("neg", [P, TPC, E])
        score = sb("score", [P, TPC, E])
        biased = sb("biased", [P, TPC, E])
        above = sb("above", [P, TPC, E, E])
        equal = sb("equal", [P, TPC, E, E])
        rank = sb("rank", [P, TPC, E])
        weight = sb("weight", [P, TPC, E])
        wrest = sb("wrest", [P, TPC, E])
        wparts = sb("wparts", [P, TPC, 3, E], BF16)
        wrows = sb("wrows", [3 * E, 2, CH], BF16)
        xs = sb("xs", [P, 2, KT, CH], BF16)
        hid = sb("hid", [P, 2, NHT, CH], BF16)
        hsq = sb("hsq", [P, 2, NHT, CH], BF16)
        shid = sb("shid", [P, NHT, CH])
        shsq = sb("shsq", [P, NHT, CH])
        eout = sb("eout", [P, 2, TPC, C], BF16)
        sout = sb("sout", [P, TPC, C])

        sp_passed = sem("sp_passed2")
        dve_passed = sem("dve_passed2")
        small = sem("small")
        cast = sem("cast")
        big = sem("big")
        pick_ready = sem("pick_ready")
        x_loaded = [sem("xl0"), sem("xl1")]
        y_loaded = [sem("yl0"), sem("yl1")]
        out_stored = [sem("os0"), sem("os1")]
        pre_psum = sem("pre_psum")
        pre_ready = sem("pre_ready")
        stats_done = sem("stats_done2")
        mv_ready = sem("mv_ready2")
        eps_set = sem("eps_set")
        std_ready = sem("std_ready2")
        rstd_ready = sem("rstd_ready2")
        xn_ready = sem("xn_ready2")
        route = sem("route")
        weights_split = sem("weights_split")
        wparts_ready = sem("wparts_ready")
        scale_psum = sem("scale_psum")
        xs_ready = sem("xs_ready")
        up_psum = sem("up_psum")
        hid_ready = sem("hid_ready")
        hsq_ready = sem("hsq_ready")
        down_psum = sem("down_psum")
        eout_ready = sem("eout_ready")
        added = sem("added")

        UP = [psum[:, m, :] for m in range(NHT)]
        DN = psum[:, 3:5, :]
        DNT = DN.rearrange("p b (t c) -> p (b t) c", c=C)
        SCL = psum[:, 5, :]
        PRE = psum[:, 6:8, :]
        PRET = PRE.rearrange("p b (t c) -> p (b t) c", c=C)
        PRE_STEPS = 6
        ROUTE_STEPS = 9
        block = ctx.enter_context(nc.Block())

        @block.sync
        def _(sp):
            def load(i, p):
                n = 2 * i + p
                sp.dma_start(yb[:, p], y_all[:, bass.ds(n * TPC, TPC), :]).then_inc(y_loaded[p], 16)
                sp.dma_start(acc[:, p], x_ch[bass.ds(n, 1)].rearrange("o p t d -> p (o t) d")
                             ).then_inc(x_loaded[p], 16)

            def store(i, p):
                n = 2 * i + p
                wait_alone(sp, added, SLOTS * (n + 1), sp_passed)
                sp.dma_start(out_ch[bass.ds(n, 1)].rearrange("o p t d -> p (o t) d"), acc[:, p]
                             ).then_inc(out_stored[p], 16)
                wait_alone(sp, out_stored[p], 16 * (i + 1), sp_passed)

            load(0, 0)
            for dst, src in ((wov, wov_t), (wou, wou_t), (gate, gate_t), (bias, bias_b), (lower, tri),
                             (pickf, sel)):
                sp.dma_start(dst[:], src).then_inc(small, 16)
            load(0, 1)
            sp.dma_start(swup[:], swup_t).then_inc(big, 16)
            sp.dma_start(swdn[:], swdn_t).then_inc(big, 16)
            with sp.Fori(0, NCHUNK // 2 - 1) as i:
                for p in range(2):
                    store(i, p)
                    load(i + 1, p)
            for p in range(2):
                store(NCHUNK // 2 - 1, p)

        @block.tensor
        def _(pe):
            def pre_start(n, step):
                wait_from_one(pe, pre_ready, PRE_STEPS * n + step)

            def turn_y(i, p):
                n = 2 * i + p
                pre_start(n, 0)
                pe.wait_ge(y_loaded[p], 16 * (i + 1))
                for k in range(KT):
                    for t in range(TPC):
                        last = pe.transpose(PRE[:, k, t * P:(t + 1) * P], yb[:, p, t, k * P:(k + 1) * P],
                                            identf[:])
                last.then_inc(pre_psum, 1)

            def project_down(n):
                pre_start(n, 1)
                for k in range(KT):
                    last = pe.matmul(PRE[0:RANK, 0, :], wov[:, k, :], ybt[:, k, :],
                                     start=k == 0, stop=k == KT - 1)
                last.then_inc(pre_psum, 1)

            def project_up(n):
                pre_start(n, 2)
                for t in range(TPC):
                    last = pe.matmul(PRET[:, t, :], zt[:, t * P:(t + 1) * P], wou[:], start=True, stop=True)
                last.then_inc(pre_psum, 1)

            def turn_x(n):
                pre_start(n, 3)
                pe.wait_ge(xn_ready, n + 1)
                for k in range(KT):
                    for t in range(TPC):
                        last = pe.transpose(PRE[:, k, t * P:(t + 1) * P], xn[:, t, k * P:(k + 1) * P],
                                            identf[:])
                last.then_inc(pre_psum, 1)

            def gate_logits(n, p):
                pre_start(n, 4)
                for t in range(TPC):
                    for k in range(KT):
                        last = pe.matmul(PRE[:, 0, t * E:(t + 1) * E], xnt[:, p, k, t * P:(t + 1) * P],
                                         gate[:, k, :], start=k == 0, stop=k == KT - 1)
                last.then_inc(pre_psum, 1)

            def turn_weights(n):
                pre_start(n, 5)
                pe.wait_ge(wparts_ready, n + 1)
                rows = PRE[0:3 * E, 1, :].bitcast(BF16)
                for t in range(TPC):
                    last = pe.transpose(rows[:, t * P:(t + 1) * P],
                                        wparts[:, t].rearrange("p a e -> p (a e)"), identb[:])
                last.then_inc(pre_psum, 1)

            def spread(n, p, e):
                if e == 0:
                    pe.wait_ge(pre_ready, PRE_STEPS * (n + 1))
                wait_from_one(pe, xs_ready, E * n + e)
                pe.matmul(SCL, pick[:, e, :], wrows[:, p, :], start=True, stop=True).then_inc(scale_psum, 1)

            def up(n, p, s):
                if s < E:
                    pe.wait_ge(xs_ready, E * n + s + 1)
                for m in range(NHT):
                    wait_from_one(pe, hid_ready, NHT * (SLOTS * n + s - 1) + m + 1)
                    for k in range(KT):
                        cols = slice(m * P, m * P + HT[m])
                        w = wup[:, s, k, cols] if s < E else swup[:, k, cols]
                        r = xs[:, s % 2, k, :] if s < E else xnt[:, p, k, :]
                        last = pe.matmul(UP[m][0:HT[m], :], w, r, start=k == 0, stop=k == KT - 1)
                    last.then_inc(up_psum, 1)

            def down(n, s):
                pe.wait_ge(hsq_ready, SLOTS * n + s + 1)
                wait_from_one(pe, eout_ready, SLOTS * n + s)
                for t in range(TPC):
                    for m in range(NHT):
                        h = (hsq[0:HT[m], s % 2, m] if s < E else shsq[0:HT[m], m])[:, t * P:(t + 1) * P]
                        w = wdn[0:HT[m], s, m, :] if s < E else swdn[0:HT[m], m, :]
                        last = pe.matmul(DNT[:, t, :], h, w, start=m == 0, stop=m == NHT - 1)
                last.then_inc(down_psum, 1)

            def chunk(i, p, more=True):
                n = 2 * i + p
                ni, np_ = i + p, 1 - p
                for s in range(SLOTS):
                    if s + 2 < E:
                        spread(n, p, s + 2)
                    elif more and s + 2 >= SLOTS:
                        spread(n + 1, np_, s + 2 - SLOTS)
                    if s + 1 < SLOTS:
                        up(n, p, s + 1)
                    elif more:
                        up(n + 1, np_, 0)
                    if more:
                        if s == 0:
                            turn_y(ni, np_)
                        if s == 1:
                            project_down(n + 1)
                        if s == 2:
                            project_up(n + 1)
                        if s == 4:
                            turn_x(n + 1)
                        if s == 5:
                            gate_logits(n + 1, np_)
                        if s == 6:
                            turn_weights(n + 1)
                    down(n, s)

            pe.wait_ge(small, 6 * 16)
            turn_y(0, 0)
            project_down(0)
            project_up(0)
            turn_x(0)
            gate_logits(0, 0)
            turn_weights(0)
            pe.wait_ge(pick_ready, 1)
            spread(0, 0, 0)
            spread(0, 0, 1)
            pe.wait_ge(cast, 32)
            pe.wait_ge(big, 32)
            up(0, 0, 0)
            with pe.Fori(0, NCHUNK // 2 - 1) as i:
                chunk(i, 0)
                chunk(i, 1)
            chunk(NCHUNK // 2 - 1, 0)
            chunk(NCHUNK // 2 - 1, 1, more=False)

        @block.scalar
        def _(act):
            def pre_copy(n, step, dst, src):
                act.wait_ge(pre_psum, PRE_STEPS * n + step + 1)
                act.activation(dst, src, ACT.Copy).then_inc(pre_ready, 1)

            def deviation(n):
                act.wait_ge(mv_ready, n + 1)
                act.activation(std[:], mv[:, :, 1], ACT.Sqrt, bias=eps[:]).then_inc(std_ready, 1)

            def gate_exp(n):
                act.wait_ge(pre_psum, PRE_STEPS * n + 5)
                wait_from_one(act, wparts_ready, n)
                act.activation(neg[:], PRE[:, 0, 0:TPC * E].rearrange("p (t e) -> p t e", e=E), ACT.Exp,
                               scale=-1.0).then_inc(pre_ready, 1)

            def relu(n, s):
                u = SLOTS * n + s
                for m in range(NHT):
                    act.wait_ge(up_psum, NHT * u + m + 1)
                    if m == 0:
                        wait_from_one(act, hsq_ready, u - 1)
                    dst = hid[0:HT[m], s % 2, m] if s < E else shid[0:HT[m], m]
                    act.activation(dst, UP[m][0:HT[m], :], ACT.Relu).then_inc(hid_ready, 1)

            def round_out(n, s):
                u = SLOTS * n + s
                act.wait_ge(down_psum, u + 1)
                wait_from_one(act, added, u - 1 if s else u)
                act.activation(eout[:, s % 2] if s < E else sout[:], DNT, ACT.Copy).then_inc(eout_ready, 1)

            def chunk(i, p, more=True):
                n = 2 * i + p
                for s in range(SLOTS):
                    if s + 1 < SLOTS:
                        relu(n, s + 1)
                    elif more:
                        relu(n + 1, 0)
                    if more:
                        if s == 0:
                            pre_copy(n + 1, 0, ybt[:], PRE)
                        if s == 1:
                            pre_copy(n + 1, 1, zt[:], PRE[0:RANK, 0, :])
                        if s == 3:
                            deviation(n + 1)
                        if s == 4:
                            pre_copy(n + 1, 3, xnt[:, 1 - p], PRE)
                        if s == 5:
                            gate_exp(n + 1)
                    round_out(n, s)

            pre_copy(0, 0, ybt[:], PRE)
            pre_copy(0, 1, zt[:], PRE[0:RANK, 0, :])
            act.wait_ge(eps_set, 1)
            deviation(0)
            pre_copy(0, 3, xnt[:, 0], PRE)
            gate_exp(0)
            relu(0, 0)
            with act.Fori(0, NCHUNK // 2 - 1) as i:
                chunk(i, 0)
                chunk(i, 1)
            chunk(NCHUNK // 2 - 1, 0)
            chunk(NCHUNK // 2 - 1, 1, more=False)

        @block.vector
        def _(dve):
            def residual_norm(i, p):
                n = 2 * i + p
                dve.wait_ge(pre_psum, PRE_STEPS * n + 3)
                dve.wait_ge(x_loaded[p], 16 * (i + 1))
                dve.tensor_tensor(acc[:, p], acc[:, p], PRET, ALU.add).then_inc(pre_ready, 1)
                dve.wait_ge(pre_ready, PRE_STEPS * n + 3)
                for t in range(TPC):
                    last = dve.bn_stats(stats[:, t, :], acc[:, p, t, :])
                last.then_inc(stats_done, 1)
                wait_alone(dve, stats_done, n + 1, dve_passed)
                for t in range(TPC):
                    last = dve.bn_aggr(mv[:, t, :], stats[:, t, :])
                last.then_inc(mv_ready, 1)

            def normalise(n, p):
                dve.wait_ge(std_ready, n + 1)
                dve.reciprocal(rstd[:], std[:]).then_inc(rstd_ready, 1)
                dve.wait_ge(rstd_ready, n + 1)
                for t in range(TPC):
                    last = dve.tensor_scalar(xn[:, t, :], acc[:, p, t, :], mv[:, t, 0:1],
                                             rstd[:, t:t + 1], ALU.subtract, ALU.mult)
                last.then_inc(xn_ready, 1)

            def routing(n):
                count = [ROUTE_STEPS * n]

                def then(ins):
                    count[0] = count[0] + 1
                    ins.then_inc(route, 1)
                    dve.wait_ge(route, count[0])

                dve.wait_ge(pre_ready, PRE_STEPS * n + 5)
                then(dve.tensor_scalar(neg[:], neg[:], 1.0, None, ALU.add))
                then(dve.reciprocal(score[:], neg[:]))
                then(dve.tensor_tensor(biased[:], score[:],
                                       bias[:].unsqueeze(1).to_broadcast([P, TPC, E]), ALU.add))
                other = biased[:].unsqueeze(2).to_broadcast([P, TPC, E, E])
                own = biased[:].unsqueeze(3).to_broadcast([P, TPC, E, E])
                dve.tensor_tensor(above[:], other, own, ALU.is_gt)
                then(dve.tensor_tensor(equal[:], other, own, ALU.is_equal))
                low = lower[:].rearrange("p (a b) -> p a b", b=E).unsqueeze(1).to_broadcast([P, TPC, E, E])
                then(dve.tensor_tensor(equal[:], equal[:], low, ALU.mult))
                then(dve.tensor_tensor(above[:], above[:], equal[:], ALU.add))
                then(dve.tensor_reduce(rank[:], above[:], AX.X, ALU.add))
                then(dve.scalar_tensor_tensor(out=weight[:], in0=rank[:], scalar=2.0, in1=score[:],
                                              op0=ALU.is_lt, op1=ALU.mult))
                then(dve.tensor_copy(wparts[:, :, 0, :], weight[:]))
                assert ROUTE_STEPS == 9

            def split_weights(n):
                dve.tensor_tensor(wrest[:], weight[:], wparts[:, :, 0, :], ALU.subtract
                                  ).then_inc(weights_split, 1)
                dve.wait_ge(weights_split, 2 * n + 1)
                dve.tensor_copy(wparts[:, :, 1, :], wrest[:]).then_inc(weights_split, 1)
                dve.wait_ge(weights_split, 2 * n + 2)
                dve.tensor_tensor(wparts[:, :, 2, :], wrest[:], wparts[:, :, 1, :], ALU.subtract
                                  ).then_inc(wparts_ready, 1)

            def copy_weights(n, p):
                dve.wait_ge(pre_psum, PRE_STEPS * n + 6)
                dve.tensor_copy(wrows[:, p, :], PRE[0:3 * E, 1, :].bitcast(BF16)[:, 0:CH]
                                ).then_inc(pre_ready, 1)

            def scale_x(n, p, e):
                dve.wait_ge(scale_psum, E * n + e + 1)
                if e > 1:
                    dve.wait_ge(up_psum, NHT * (SLOTS * n + e - 1))
                else:
                    wait_from_one(dve, up_psum, NHT * (SLOTS * (n - 1) + E - 1 + e))
                dve.tensor_tensor(xs[:, e % 2], xnt[:, p], SCL.unsqueeze(1).to_broadcast([P, KT, CH]),
                                  ALU.mult).then_inc(xs_ready, 1)

            def square(n, s):
                u = SLOTS * n + s
                src, dst = (hid[:, s % 2], hsq[:, s % 2]) if s < E else (shid[:], shsq[:])
                dve.wait_ge(hid_ready, NHT * (u + 1))
                wait_from_one(dve, down_psum, u - 1)
                dve.tensor_tensor(dst[:, 0:2], src[:, 0:2], src[:, 0:2], ALU.mult)
                dve.tensor_tensor(dst[0:HT[2], 2], src[0:HT[2], 2], src[0:HT[2], 2], ALU.mult
                                  ).then_inc(hsq_ready, 1)

            def chunk(i, p, more=True):
                n = 2 * i + p
                ni, np_ = i + p, 1 - p
                for s in range(SLOTS):
                    if s + 2 < E:
                        scale_x(n, p, s + 2)
                    elif more and s + 2 >= SLOTS:
                        scale_x(n + 1, np_, s + 2 - SLOTS)
                    if s + 1 < SLOTS:
                        square(n, s + 1)
                    elif more:
                        square(n + 1, 0)
                    if more:
                        if s == 2:
                            residual_norm(ni, np_)
                        if s == 3:
                            normalise(n + 1, np_)
                        if s == 5:
                            routing(n + 1)
                            split_weights(n + 1)
                        if s == 6:
                            copy_weights(n + 1, np_)

            dve.memset(eps[:], EPS).then_inc(eps_set, 1)
            dve.wait_ge(small, 6 * 16)
            dve.tensor_copy(pick[:], pickf[:]).then_inc(pick_ready, 1)
            residual_norm(0, 0)
            normalise(0, 0)
            routing(0)
            split_weights(0)
            copy_weights(0, 0)
            scale_x(0, 0, 0)
            scale_x(0, 0, 1)
            square(0, 0)
            with dve.Fori(0, NCHUNK // 2 - 1) as i:
                chunk(i, 0)
                chunk(i, 1)
            chunk(NCHUNK // 2 - 1, 0)
            chunk(NCHUNK // 2 - 1, 1, more=False)

        @block.gpsimd
        def _(pool):
            def add_out(n, p, s):
                u = SLOTS * n + s
                pool.wait_ge(eout_ready, u + 1)
                wait_from_one(pool, added, u)
                pool.tensor_tensor(acc[:, p], acc[:, p], eout[:, s % 2] if s < E else sout[:], ALU.add
                                   ).then_inc(added, 1)

            def chunk(i, p, more=True):
                n = 2 * i + p
                for s in range(SLOTS):
                    add_out(n, p, s)

            pool.dma_start(wup[:], wup_t).then_inc(cast, 16)
            pool.dma_start(wdn[:], wdn_t).then_inc(cast, 16)
            with pool.Fori(0, NCHUNK // 2 - 1) as i:
                chunk(i, 0)
                chunk(i, 1)
            chunk(NCHUNK // 2 - 1, 0)
            chunk(NCHUNK // 2 - 1, 1, more=False)


def kernel(**inputs):
    import numpy as np
    import concourse.bacc as bacc
    from concourse.bass_utils import run_bass_kernel_spmd

    def a(name):
        return np.asarray(inputs[name])

    def by_partition(w):
        k, n = w.shape
        tiles = -(-k // P)
        full = np.zeros((tiles * P, n), w.dtype)
        full[:k] = w
        return full.reshape(tiles, P, n).transpose(1, 0, 2)

    experts = range(E)
    eye3 = np.zeros((3, E, E, P), np.float32)
    for e in experts:
        eye3[:, e, e, :] = 1.0
    arrays = {
        "x": a("L0_attn_x"),
        "wv_t": by_partition(a("L0_attn_W_qkv_v").T),
        "wu_t": a("L0_attn_W_qkv_u").T,
        "wov_t": by_partition(a("L0_attn_W_o_v").T),
        "wou_t": a("L0_attn_W_o_u").T,
        "gate_t": by_partition(a("L0_ffn_gate_w").T),
        "bias_b": np.tile(a("L0_ffn_expert_bias")[None, :], (P, 1)),
        "wup_t": np.stack([by_partition(a("L0_ffn_w_up")[e].T) for e in experts], 1),
        "wdn_t": np.stack([by_partition(a("L0_ffn_w_down")[e].T) for e in experts], 1),
        "swup_t": by_partition(a("L0_ffn_shared_w_up").T),
        "swdn_t": by_partition(a("L0_ffn_shared_w_down").T),
        "ident": np.eye(P, dtype=np.float32),
        "tri": np.tile(np.tril(np.ones((E, E), np.float32), -1).reshape(1, E * E), (P, 1)),
        "sel": eye3.reshape(3 * E, E, P),
    }
    arrays = {k: np.ascontiguousarray(v) for k, v in arrays.items()}
    nc = bacc.Bacc("TRN2", target_bir_lowering=False, num_devices=1)
    args = [nc.dram_tensor(k, v.shape, mybir.dt.from_np(v.dtype), kind="ExternalInput").ap()
            for k, v in arrays.items()]
    args.append(nc.dram_tensor("out", (B, T, C), F32, kind="ExternalOutput").ap())
    build(nc, *args)
    r = run_bass_kernel_spmd(nc, [arrays], core_ids=[0])
    return r.results[0]["out"]
```

```python
from contextlib import ExitStack

import concourse.bass as bass
from concourse import mybir

P = 128
B, T, C = 2, 2048, 256
NH, HD = 16, 16
RANK = 64
E, HID = 8, 352
EPS = 1e-5
SCALE = HD ** -0.5

CH = 512
TPC = CH // P
KT = C // P
NCHUNK = B * T // CH
HG = 4
NG = B * NH // HG
QPG = T // CH
UNITS = NG * QPG
ST = T // P
NPROD = 6
KROWS = NPROD * HD
QPART = (0, 0, 0, 1, 1, 2)
KPART = (0, 1, 2, 0, 1, 0)
ROWS = KROWS + 3
VW = HD + 1
HT = [P, P, HID - 2 * P]
NHT = len(HT)
SLOTS = E + 1

ALU = mybir.AluOpType
ACT = mybir.ActivationFunctionType
AX = mybir.AxisListType
F32 = mybir.dt.float32
BF16 = mybir.dt.bfloat16


def wait_from_one(eng, sem, value):
    if not isinstance(value, int) or value > 0:
        eng.wait_ge(sem, value)


def wait_alone(eng, sem, value, passed):
    eng.wait_ge(sem, value)
    if not isinstance(value, int):
        eng.sem_inc(passed, 1)


def build(nc, x, wv_t, wu_t, wov_t, wou_t, gate_t, bias_b, wup_t, wdn_t, swup_t, swdn_t,
          ident, tri, sel, out):
    parts_d = nc.dram_tensor("parts_d", [3, 2 * C, B * T], BF16).ap()
    v_d = nc.dram_tensor("v_d", [NG, P, ST, HG * VW], F32).ap()
    x_ch = x.rearrange("b (c t p) d -> (b c) p t d", p=P, t=TPC)
    out_ch = out.rearrange("b (c t p) d -> (b c) p t d", p=P, t=TPC)

    with ExitStack() as ctx:
        psum = ctx.enter_context(nc.psum_tensor("psum", [P, 8, CH], F32))
        identf = ctx.enter_context(nc.sbuf_tensor("identf", [P, P], F32))
        identb = ctx.enter_context(nc.sbuf_tensor("identb", [P, P], BF16))
        y_all = ctx.enter_context(nc.sbuf_tensor("y_all", [P, B * T // P, C], F32))
        project_qkv(nc, psum, identf, identb, x_ch, wv_t, wu_t, ident, parts_d, v_d)
        attend(nc, psum, identf, identb, y_all, parts_d, v_d)
        mix_experts(nc, psum, identf, identb, y_all, x_ch, out_ch, wov_t, wou_t, gate_t, bias_b,
                    wup_t, wdn_t, swup_t, swdn_t, tri, sel)


def project_qkv(nc, psum, identf, identb, x_ch, wv_t, wu_t, ident, parts_d, v_d):
    with ExitStack() as ctx:
        def sb(name, shape, dt=F32):
            return ctx.enter_context(nc.sbuf_tensor(name, shape, dt))

        def sem(name):
            return ctx.enter_context(nc.semaphore(name))

        wv = sb("wv", [P, KT, RANK])
        wu = sb("wu", [RANK, 3 * C])
        xin = sb("xin", [P, 2, TPC, C])
        stats = sb("stats", [P, TPC, 6])
        mv = sb("mv", [P, TPC, 2])
        eps = sb("eps", [P, 1])
        std = sb("std", [P, TPC])
        rstd = sb("rstd", [P, TPC])
        xn = sb("xn", [P, 2, TPC, C])
        xnt = sb("xnt", [P, KT, CH])
        at = sb("at", [RANK, CH])
        parts = sb("parts", [P, 2, 3, 2 * KT, CH], BF16)
        rest = sb("rest", [P, 2 * KT, CH])
        vst = sb("vst", [P, 2, TPC, NH, VW])

        sp_passed = sem("sp_passed")
        dve_passed = sem("dve_passed")
        weights = sem("weights")
        consts = sem("consts")
        x_loaded = [sem("x_loaded0"), sem("x_loaded1")]
        stats_done = sem("stats_done")
        mv_ready = sem("mv_ready")
        std_ready = sem("std_ready")
        rstd_ready = sem("rstd_ready")
        xn_ready = sem("xn_ready")
        xt_psum = sem("xt_psum")
        xt_ready = sem("xt_ready")
        at_psum = sem("at_psum")
        at_ready = sem("at_ready")
        qk_psum = sem("qk_psum")
        v_psum = sem("v_psum")
        part0_ready = sem("part0_ready")
        rest_ready = sem("rest_ready")
        part1_ready = sem("part1_ready")
        part2_ready = sem("part2_ready")
        v_ready = sem("v_ready")
        parts_stored = [sem("parts_stored0"), sem("parts_stored1")]
        v_stored = [sem("v_stored0"), sem("v_stored1")]

        XT, AT, QK, VB = psum[:, 0:2, :], psum[0:RANK, 0, :], psum[:, 3:7, :], (psum[:, 7, :], psum[:, 2, :])
        block = ctx.enter_context(nc.Block())

        @block.sync
        def _(sp):
            def load(i, p):
                sp.dma_start(xin[:, p], x_ch[bass.ds(2 * i + p, 1)].rearrange("o p t d -> p (o t) d")
                             ).then_inc(x_loaded[p], 16)

            def store(i, p):
                n = 2 * i + p
                wait_alone(sp, part2_ready, n + 1, sp_passed)
                for j in range(3):
                    sp.dma_start(parts_d[j, :, bass.ds(n * CH, CH)].rearrange("(m p) t -> p m t", p=P),
                                 parts[:, p, j]).then_inc(parts_stored[p], 16)
                wait_alone(sp, v_ready, n + 1, sp_passed)
                for g in range(NH // HG):
                    group = (n // QPG) * (NH // HG) + g
                    sp.dma_start(v_d[bass.ds(group, 1), :, bass.ds((n % QPG) * TPC, TPC), :]
                                 .rearrange("o p t c -> p (o t) c"),
                                 vst[:, p, :, g * HG:(g + 1) * HG, :].rearrange("p t h c -> p t (h c)")
                                 ).then_inc(v_stored[p], 16)

            load(0, 0)
            sp.dma_start(identf[:], ident).then_inc(weights, 16)
            sp.dma_start(wv[:], wv_t).then_inc(weights, 16)
            sp.dma_start(wu[:], wu_t).then_inc(weights, 16)
            load(0, 1)
            def pair(i):
                for p in range(2):
                    wait_alone(sp, xn_ready, 2 * i + p + 1, sp_passed)
                    load(i + 1, p)
                    store(i, p)

            pair(0)
            with sp.Fori(1, NCHUNK // 2 - 1) as i:
                pair(i)
            for p in range(2):
                store(NCHUNK // 2 - 1, p)
            for p in range(2):
                wait_alone(sp, parts_stored[p], 3 * 16 * NCHUNK // 2, sp_passed)
                wait_alone(sp, v_stored[p], (NH // HG) * 16 * NCHUNK // 2, sp_passed)

        @block.vector
        def _(dve):
            def normalise(i, p):
                n = 2 * i + p
                dve.wait_ge(x_loaded[p], 16 * (i + 1))
                wait_from_one(dve, xn_ready, n)
                for t in range(TPC):
                    last = dve.bn_stats(stats[:, t, :], xin[:, p, t, :])
                last.then_inc(stats_done, 1)
                wait_alone(dve, stats_done, n + 1, dve_passed)
                for t in range(TPC):
                    last = dve.bn_aggr(mv[:, t, :], stats[:, t, :])
                last.then_inc(mv_ready, 1)
                dve.wait_ge(std_ready, n + 1)
                dve.reciprocal(rstd[:], std[:]).then_inc(rstd_ready, 1)
                dve.wait_ge(rstd_ready, n + 1)
                wait_from_one(dve, xt_psum, n - 1)
                for t in range(TPC):
                    last = dve.tensor_scalar(xn[:, p, t, :], xin[:, p, t, :], mv[:, t, 0:1],
                                             rstd[:, t:t + 1], ALU.subtract, ALU.mult)
                last.then_inc(xn_ready, 1)

            def take_rest(i, p):
                n = 2 * i + p
                dve.wait_ge(part0_ready, n + 1)
                wait_from_one(dve, part2_ready, n)
                dve.tensor_tensor(rest[:], QK, parts[:, p, 0], ALU.subtract).then_inc(rest_ready, 1)

            dve.memset(eps[:], EPS)
            dve.memset(vst[:, 0, :, :, HD:VW], 1.0)
            dve.memset(vst[:, 1, :, :, HD:VW], 1.0).then_inc(consts, 1)
            dve.wait_ge(weights, 48)
            dve.tensor_copy(identb[:], identf[:]).then_inc(consts, 1)
            normalise(0, 0)
            normalise(0, 1)
            take_rest(0, 0)
            with dve.Fori(1, NCHUNK // 2) as i:
                normalise(i, 0)
                take_rest(i - 1, 1)
                normalise(i, 1)
                take_rest(i, 0)
            take_rest(NCHUNK // 2 - 1, 1)

        @block.gpsimd
        def _(pool):
            def last_part(i, p):
                n = 2 * i + p
                pool.wait_ge(part1_ready, n + 1)
                pool.tensor_tensor(parts[:, p, 2], rest[:], parts[:, p, 1], ALU.subtract
                                   ).then_inc(part2_ready, 1)

            last_part(0, 0)
            with pool.Fori(1, NCHUNK // 2) as i:
                last_part(i - 1, 1)
                last_part(i, 0)
            last_part(NCHUNK // 2 - 1, 1)

        @block.tensor
        def _(pe):
            def transpose_x(i, p):
                n = 2 * i + p
                pe.wait_ge(xn_ready, n + 1)
                wait_from_one(pe, xt_ready, n)
                for k in reversed(range(KT)):
                    if k == 0:
                        wait_from_one(pe, at_ready, n)
                    for t in range(TPC):
                        last = pe.transpose(XT[:, k, t * P:(t + 1) * P],
                                            xn[:, p, t, k * P:(k + 1) * P], identf[:])
                last.then_inc(xt_psum, 1)

            def project_down(n):
                pe.wait_ge(xt_ready, n + 1)
                for k in range(KT):
                    last = pe.matmul(AT, wv[:, k, :], xnt[:, k, :], start=k == 0, stop=k == KT - 1)
                last.then_inc(at_psum, 1)

            def project_up(n):
                pe.wait_ge(at_ready, n + 1)
                wait_from_one(pe, rest_ready, n)
                for m in range(2 * KT):
                    last = pe.matmul(QK[:, m, :], wu[:, m * P:(m + 1) * P], at[:], start=True, stop=True)
                last.then_inc(qk_psum, 1)
                wait_from_one(pe, v_ready, n)
                for t in range(TPC):
                    last = pe.matmul(VB[t // 2][:, (t % 2) * C:(t % 2 + 1) * C], at[:, t * P:(t + 1) * P],
                                     wu[:, 2 * C:3 * C], start=True, stop=True)
                last.then_inc(v_psum, 1)

            pe.wait_ge(weights, 48)
            def pair(i):
                for p in range(2):
                    project_down(2 * i + p)
                    transpose_x(i + p, 1 - p)
                    project_up(2 * i + p)

            transpose_x(0, 0)
            pair(0)
            with pe.Fori(1, NCHUNK // 2 - 1) as i:
                pair(i)
            i = NCHUNK // 2 - 1
            project_down(2 * i)
            transpose_x(i, 1)
            project_up(2 * i)
            project_down(2 * i + 1)
            project_up(2 * i + 1)

        @block.scalar
        def _(act):
            def deviation(n):
                act.wait_ge(mv_ready, n + 1)
                act.activation(std[:], mv[:, :, 1], ACT.Sqrt, bias=eps[:]).then_inc(std_ready, 1)

            def copy_xt(n):
                act.wait_ge(xt_psum, n + 1)
                wait_from_one(act, at_psum, n)
                act.activation(xnt[:], XT, ACT.Copy).then_inc(xt_ready, 1)

            def copy_at(n):
                act.wait_ge(at_psum, n + 1)
                wait_from_one(act, v_psum, n)
                act.activation(at[:], AT, ACT.Copy).then_inc(at_ready, 1)

            def copy_qkv(i, p):
                n = 2 * i + p
                act.wait_ge(qk_psum, n + 1)
                wait_from_one(act, parts_stored[p], 48 * i)
                act.activation(parts[:, p, 0], QK, ACT.Copy).then_inc(part0_ready, 1)
                act.wait_ge(v_psum, n + 1)
                wait_from_one(act, v_stored[p], 64 * i)
                for j in range(2):
                    last = act.activation(vst[:, p, 2 * j:2 * j + 2, :, 0:HD],
                                          VB[j].rearrange("p (t h c) -> p t h c", t=2, h=NH), ACT.Copy)
                last.then_inc(v_ready, 1)
                act.wait_ge(rest_ready, n + 1)
                act.activation(parts[:, p, 1], rest[:], ACT.Copy).then_inc(part1_ready, 1)

            act.wait_ge(consts, 1)
            deviation(0)
            copy_xt(0)
            deviation(1)

            def pair(i):
                for p in range(2):
                    copy_at(2 * i + p)
                    copy_xt(2 * i + p + 1)
                    copy_qkv(i, p)
                    deviation(2 * i + p + 2)

            pair(0)
            with act.Fori(1, NCHUNK // 2 - 1) as i:
                pair(i)
            i = NCHUNK // 2 - 1
            copy_at(2 * i)
            copy_xt(2 * i + 1)
            copy_qkv(i, 0)
            copy_at(2 * i + 1)
            copy_qkv(i, 1)


def attend(nc, psum, identf, identb, y_all, parts_d, v_d):
    with ExitStack() as ctx:
        def sb(name, shape, dt=F32):
            return ctx.enter_context(nc.sbuf_tensor(name, shape, dt))

        def sem(name):
            return ctx.enter_context(nc.semaphore(name))

        RING = 2 * T
        kst = sb("kst", [ROWS, HG, RING], BF16)
        qst = sb("qst", [ROWS, HG, RING], BF16)
        vcur = sb("vcur", [P, ST, HG, VW])
        PS = 4
        probs = sb("probs", [P, PS, HG, CH])
        SC = T // CH
        mx = sb("mx", [P, 2, HG, SC])
        negmax = sb("negmax", [P, 2, HG])
        mrest = sb("mrest", [P, 2, HG])
        mparts = sb("mparts", [P, 2, 3, HG], BF16)
        mrows = sb("mrows", [3 * HG, 2, P], BF16)
        yt = sb("yt", [P, CH])
        rsum = sb("rsum", [P, TPC, HG])

        sp_passed = sem("sp_passed1")
        pool_passed = sem("pool_passed1")
        ones_set = sem("ones_set")
        acc_zero = sem("acc_zero")
        stacks_loaded = sem("stacks_loaded")
        v_loaded = sem("v_loaded")
        ring_filled = sem("ring_filled")
        ring_used = sem("ring_used")
        negmax_ready = sem("negmax_ready")
        split_done = sem("split_done")
        mparts_ready = sem("mparts_ready")
        mrows_placed = sem("mrows_placed")
        scores_ready = sem("scores_ready")
        probs_ready = sem("probs_ready")
        pv_done = sem("pv_done")
        yt_ready = sem("yt_ready")
        rsum_ready = sem("rsum_ready")

        SB = [psum[:, h, :] for h in range(HG)]
        ACC = psum[:, 4, :]
        RB = [psum[:, 5 + b, :] for b in range(3)]
        SCORES, MAXIMA, OUTPUTS = range(3)

        def ring_plan(first=False, tiles=TPC, last=False):
            plan = []
            for j in range(ST):
                step = []
                if j % 4 == 1 and j // 4 <= tiles and not last:
                    step.append(MAXIMA)
                if j == 3 and not first:
                    step.append(OUTPUTS)
                if j // 4 < tiles:
                    step += [SCORES] * SC
                plan.append(step)
            return plan

        PER_UNIT = sum(map(len, ring_plan()))
        AHEAD = (TPC + 1) * HG * SC + TPC
        FIRST = sum(map(len, ring_plan(first=True)))
        assert PER_UNIT % 3 == 0

        def ring_base(u):
            if isinstance(u, int) and u == 0:
                return AHEAD
            if isinstance(u, int) and u == UNITS - 1:
                return ring_base(u - 1) + sum(map(len, ring_plan(tiles=TPC - 1)))
            return AHEAD + FIRST + PER_UNIT * (u - 1)

        def ring_place(j, what, **kind):
            plan = ring_plan(**kind)
            return sum(map(len, plan[:j])) + plan[j].index(what)

        BEFORE_LAST = sum(map(len, ring_plan(tiles=TPC - 1)))
        RING_ENTRIES = ring_base(UNITS - 2) + BEFORE_LAST + 2
        STACK_DMAS = 2 * NPROD
        QT = T // P
        NQ = UNITS * TPC

        block = ctx.enter_context(nc.Block())

        @block.sync
        def _(sp):
            def load_stacks(g):
                batch, row = g // (NH // HG), (g % (NH // HG)) * HG * HD
                cols = (g % 2) * T
                for side, stack, part in ((0, qst, QPART), (1, kst, KPART)):
                    for j in range(NPROD):
                        src = parts_d[part[j], bass.ds(side * C + row, HG * HD), bass.ds(batch * T, T)]
                        sp.dma_start(stack[j * HD:(j + 1) * HD, :, bass.ds(cols, T)],
                                     src.rearrange("(h d) t -> d h t", d=HD)
                                     ).then_inc(stacks_loaded, 16)

            def load_v(g, q):
                sp.dma_start(vcur[:, q * 4:(q + 1) * 4].rearrange("p s h c -> p s (h c)"),
                             v_d[bass.ds(g, 1), :, q * 4:(q + 1) * 4].rearrange("o p s c -> p (o s) c")
                             ).then_inc(v_loaded, 16)

            def next_v(g):
                for q in range(4):
                    wait_alone(sp, pv_done, (QPG * g - 1) * ST + 4 * q + 4, sp_passed)
                    wait_alone(sp, v_loaded, 16 * (4 * g + q), sp_passed)
                    load_v(g, q)

            load_stacks(0)
            for q in range(4):
                load_v(0, q)
                sp.wait_ge(v_loaded, 16 * (q + 1))
            sp.wait_ge(stacks_loaded, 16 * STACK_DMAS)
            load_stacks(1)
            with sp.Fori(1, NG - 1) as g:
                next_v(g)
                wait_alone(sp, scores_ready, HG * ST * QPG * g, sp_passed)
                wait_alone(sp, stacks_loaded, 16 * STACK_DMAS * (g + 1), sp_passed)
                load_stacks(g + 1)
            next_v(NG - 1)

        @block.tensor
        def _(pe):
            def score_max(q, h, c, bank, entry):
                wait_from_one(pe, ring_used, entry - 2)
                col = (q % (2 * QT)) * P
                kcol = ((q // QT) % 2) * T + c * CH
                pe.matmul(bank, qst[0:KROWS, h, bass.ds(col, P)], kst[0:KROWS, h, bass.ds(kcol, CH)],
                          start=True, stop=True).then_inc(ring_filled, 1)

            def stack_wait(q):
                pe.wait_ge(stacks_loaded, 16 * STACK_DMAS * (q // QT + 1))

            def turn_maxima(q, par, bank, entry):
                pe.wait_ge(mparts_ready, q + 1)
                pe.wait_ge(ring_used, entry - 2)
                pe.transpose(bank.bitcast(BF16)[0:3 * HG, 0:P], mparts[:, par].rearrange("p a h -> p (a h)"),
                             identb[:]).then_inc(ring_filled, 1)

            def score(u, j, h):
                n = (u * ST + j) * HG + h
                wait_from_one(pe, probs_ready, n - HG + 1)
                qcol = (u % (2 * QPG)) * CH
                kcol = ((u // QPG) % 2) * T + j * P
                pe.matmul(SB[h], kst[:, h, bass.ds(kcol, P)], qst[:, h, bass.ds(qcol, CH)],
                          start=True, stop=True).then_inc(scores_ready, 1)

            def weigh(u, j):
                pe.wait_ge(probs_ready, (u * ST + j + 1) * HG)
                if j % 4 == 0:
                    pe.wait_ge(v_loaded, 16 * (4 * (u // QPG) + j // 4 + 1))
                if j == 0:
                    wait_from_one(pe, yt_ready, u)
                for h in range(HG):
                    last = pe.matmul(ACC[32 * h:32 * h + VW, :], vcur[:, j, h, :], probs[:, j % PS, h, :],
                                     start=j == 0, stop=j == ST - 1)
                last.then_inc(pv_done, 1)

            def turn_y(u, bank, entry):
                pe.wait_ge(yt_ready, u + 1)
                pe.wait_ge(ring_used, entry - 2)
                for t in range(TPC):
                    last = pe.transpose(bank[:, t * P:(t + 1) * P], yt[:, t * P:(t + 1) * P], identf[:])
                last.then_inc(ring_filled, 1)

            def unit(u, place, **kind):
                r = 0
                last = kind.get("last", False)
                base = ring_base(u)
                for j, step in enumerate(ring_plan(**kind)):
                    q = TPC * (u + 1) + 1 + j // 4
                    if j % 4 == 0 and SCORES in step:
                        stack_wait(q)
                    if j == ST - 1 and not last:
                        pe.wait_ge(mrows_placed, 16 * TPC * (u + 2))
                    if MAXIMA in step:
                        turn_maxima(q - 1, (j // 4) % 2, RB[(place + r) % 3], base + r)
                        r += 1
                    if OUTPUTS in step:
                        turn_y(u - 1, RB[(place + r) % 3], base + r)
                        r += 1
                    for h in range(HG):
                        if j < ST - 1:
                            score(u, j + 1, h)
                        elif not last:
                            score(u + 1, 0, h)
                        if SCORES in step:
                            score_max(q, j % 4, h, RB[(place + r) % 3], base + r)
                            r += 1
                    weigh(u, j)

            pe.wait_ge(ones_set, 1)
            stack_wait(0)
            r = 0
            for q in range(TPC + 1):
                for h in range(HG):
                    for c in range(SC):
                        score_max(q, h, c, RB[r % 3], r)
                        r += 1
                if q > 0:
                    turn_maxima(q - 1, (q - 1) % 2, RB[r % 3], r)
                    r += 1
            pe.wait_ge(mrows_placed, 16 * TPC)
            for h in range(HG):
                score(0, 0, h)
            pe.wait_ge(acc_zero, 1)
            unit(0, AHEAD, first=True)
            with pe.Fori(1, UNITS - 2) as u:
                unit(u, AHEAD + FIRST)
            unit(UNITS - 2, ring_base(UNITS - 2), tiles=TPC - 1)
            unit(UNITS - 1, ring_base(UNITS - 2) + BEFORE_LAST, tiles=0, last=True)
            end = RING_ENTRIES - 1
            turn_y(UNITS - 1, RB[end % 3], end)

        @block.scalar
        def _(act):
            def exponentials(u, j):
                for h in range(HG):
                    n = (u * ST + j) * HG + h
                    act.wait_ge(scores_ready, n + 1)
                    if h == 0:
                        wait_from_one(act, pv_done, u * ST + j - PS + 1)
                    act.activation(probs[:, j % PS, h, :], SB[h], ACT.Exp, scale=SCALE
                                   ).then_inc(probs_ready, 1)

            def copy_sums(u, last=False):
                act.wait_ge(pv_done, (u + 1) * ST)
                if not isinstance(u, int) or u > 0:
                    kind = {"tiles": 0, "last": True} if last else {}
                    act.wait_ge(ring_filled, ring_base(u) + ring_place(3, OUTPUTS, **kind) + 1)
                act.activation(yt[:], ACC, ACT.Copy).then_inc(yt_ready, 1)

            def unit(u, last=False):
                for j in range(ST - 1):
                    exponentials(u, j + 1)
                if not last:
                    exponentials(u + 1, 0)
                copy_sums(u, last)

            exponentials(0, 0)
            unit(0)
            with act.Fori(1, UNITS - 1) as u:
                unit(u)
            unit(UNITS - 1, last=True)

        @block.vector
        def _(dve):
            def reduce_scores(q, par, h, c, bank, entry):
                dve.wait_ge(ring_filled, entry + 1)
                dve.tensor_reduce(mx[:, par, h, c:c + 1], bank, AX.X, ALU.max).then_inc(ring_used, 1)

            def finish_maxima(q, par, entries):
                dve.wait_ge(ring_used, entries)
                wait_from_one(dve, mparts_ready, q - 1)
                dve.tensor_reduce(negmax[:, par, :], mx[:, par], AX.X, ALU.max, negate=True
                                  ).then_inc(negmax_ready, 1)

            def copy_maxima(q, par, bank, entry):
                dve.wait_ge(ring_filled, entry + 1)
                wait_from_one(dve, mrows_placed, 16 * (q - 1))
                dve.tensor_copy(mrows[:, par, :], bank.bitcast(BF16)[0:3 * HG, 0:P]).then_inc(ring_used, 1)

            def divide(u, bank, entry):
                dve.wait_ge(ring_used, entry)
                dve.wait_ge(ring_filled, entry + 1)
                heads = bank.rearrange("p (t h c) -> p t h c", t=TPC, h=HG)
                dve.reciprocal(rsum[:], heads[:, :, :, HD]).then_inc(rsum_ready, 1)
                dve.wait_ge(rsum_ready, u + 1)
                batch, group, chunk = u // (UNITS // B), (u // QPG) % (NH // HG), u % QPG
                tile = batch * (T // P) + chunk * TPC
                dst = y_all[:, bass.ds(tile, TPC), bass.ds(group * (HG * HD), HG * HD)]
                dve.tensor_tensor(dst.rearrange("p t (h c) -> p t h c", h=HG), heads[:, :, :, 0:HD],
                                  rsum[:].unsqueeze(3).to_broadcast([P, TPC, HG, HD]), ALU.mult
                                  ).then_inc(ring_used, 1)

            def unit(u, place, **kind):
                r = 0
                base = ring_base(u)
                for j, step in enumerate(ring_plan(**kind)):
                    q = TPC * (u + 1) + 1 + j // 4
                    par = (1 + j // 4) % 2
                    if MAXIMA in step:
                        copy_maxima(q - 1, 1 - par, RB[(place + r) % 3], base + r)
                        r += 1
                    if OUTPUTS in step:
                        divide(u - 1, RB[(place + r) % 3], base + r)
                        r += 1
                    if SCORES in step:
                        for c in range(SC):
                            reduce_scores(q, par, j % 4, c, RB[(place + r) % 3], base + r)
                            r += 1
                        if j % 4 == 3:
                            finish_maxima(q, par, base + r)

            dve.memset(ACC, 0.0).then_inc(acc_zero, 1)
            dve.memset(kst[KROWS:ROWS], 1.0).then_inc(ones_set, 1)
            r = 0
            for q in range(TPC + 1):
                for h in range(HG):
                    for c in range(SC):
                        reduce_scores(q, q % 2, h, c, RB[r % 3], r)
                        r += 1
                if q > 0:
                    copy_maxima(q - 1, (q - 1) % 2, RB[r % 3], r)
                    r += 1
                finish_maxima(q, q % 2, r)
            unit(0, AHEAD, first=True)
            with dve.Fori(1, UNITS - 2) as u:
                unit(u, AHEAD + FIRST)
            unit(UNITS - 2, ring_base(UNITS - 2), tiles=TPC - 1)
            unit(UNITS - 1, ring_base(UNITS - 2) + BEFORE_LAST, tiles=0, last=True)
            end = RING_ENTRIES - 1
            divide(UNITS - 1, RB[end % 3], end)

        @block.gpsimd
        def _(pool):
            def split(q, par, entry):
                wait_alone(pool, negmax_ready, q + 1, pool_passed)
                pool.tensor_copy(mparts[:, par, 0], negmax[:, par]).then_inc(split_done, 1)
                wait_alone(pool, split_done, 3 * q + 1, pool_passed)
                pool.tensor_tensor(mrest[:, par], negmax[:, par], mparts[:, par, 0], ALU.subtract
                                   ).then_inc(split_done, 1)
                wait_alone(pool, split_done, 3 * q + 2, pool_passed)
                pool.tensor_copy(mparts[:, par, 1], mrest[:, par]).then_inc(split_done, 1)
                wait_alone(pool, split_done, 3 * q + 3, pool_passed)
                pool.tensor_tensor(mparts[:, par, 2], mrest[:, par], mparts[:, par, 1], ALU.subtract
                                   ).then_inc(mparts_ready, 1)
                pool.wait_ge(ring_used, entry + 1)
                wait_from_one(pool, mrows_placed, 16 * q)
                pool.dma_start(qst[KROWS:ROWS, :, bass.ds((q % (2 * QT)) * P, P)],
                               mrows[:, par, :]).then_inc(mrows_placed, 16)

            def unit(u, **kind):
                for i in range(TPC):
                    split(TPC * (u + 1) + i, i % 2, ring_base(u) + ring_place(4 * i + 1, MAXIMA, **kind))

            for q in range(TPC):
                split(q, q % 2, HG * SC * (q + 2) + q)
            unit(0, first=True)
            with pool.Fori(1, UNITS - 2) as u:
                unit(u)
            unit(UNITS - 2, tiles=TPC - 1)
            pool.wait_ge(mrows_placed, 16 * NQ)


def mix_experts(nc, psum, identf, identb, y_all, x_ch, out_ch, wov_t, wou_t, gate_t, bias_b,
                wup_t, wdn_t, swup_t, swdn_t, tri, sel):
    with ExitStack() as ctx:
        def sb(name, shape, dt=F32):
            return ctx.enter_context(nc.sbuf_tensor(name, shape, dt))

        def sem(name):
            return ctx.enter_context(nc.semaphore(name))

        wov = sb("wov", [P, KT, RANK])
        wou = sb("wou", [RANK, C])
        gate = sb("gate", [P, KT, E])
        bias = sb("bias", [P, E])
        lower = sb("lower", [P, E * E])
        pick = sb("pick", [3 * E, E, P], BF16)
        pickf = sb("pickf", [3 * E, E, P])
        wup = sb("wup", [P, E, KT, HID], BF16)
        wdn = sb("wdn", [P, E, NHT, C], BF16)
        swup = sb("swup", [P, KT, HID])
        swdn = sb("swdn", [P, NHT, C])

        yb = sb("yb", [P, 2, TPC, C])
        xb = sb("xb", [P, 2, TPC, C])
        acc = sb("acc", [P, 2, TPC, C])
        ybt = sb("ybt", [P, KT, CH])
        zt = sb("zt", [RANK, CH])
        stats = sb("stats2", [P, TPC, 6])
        mv = sb("mv2", [P, TPC, 2])
        eps = sb("eps2", [P, 1])
        std = sb("std2", [P, TPC])
        rstd = sb("rstd2", [P, TPC])
        xn = sb("xn2", [P, TPC, C])
        xnt = sb("xnt2", [P, 2, KT, CH])
        neg = sb("neg", [P, TPC, E])
        score = sb("score", [P, TPC, E])
        biased = sb("biased", [P, TPC, E])
        above = sb("above", [P, TPC, E, E])
        equal = sb("equal", [P, TPC, E, E])
        rank = sb("rank", [P, TPC, E])
        weight = sb("weight", [P, TPC, E])
        wrest = sb("wrest", [P, TPC, E])
        wparts = sb("wparts", [P, TPC, 3, E], BF16)
        wrows = sb("wrows", [3 * E, 2, CH], BF16)
        xs = sb("xs", [P, 2, KT, CH], BF16)
        hid = sb("hid", [P, 2, NHT, CH], BF16)
        hsq = sb("hsq", [P, 2, NHT, CH], BF16)
        shid = sb("shid", [P, NHT, CH])
        shsq = sb("shsq", [P, NHT, CH])
        eout = sb("eout", [P, 2, TPC, C], BF16)
        sout = sb("sout", [P, TPC, C])

        sp_passed = sem("sp_passed2")
        dve_passed = sem("dve_passed2")
        small = sem("small")
        cast = sem("cast")
        big = sem("big")
        pick_ready = sem("pick_ready")
        x_loaded = [sem("xl0"), sem("xl1")]
        y_loaded = [sem("yl0"), sem("yl1")]
        out_stored = [sem("os0"), sem("os1")]
        pre_psum = sem("pre_psum")
        pre_ready = sem("pre_ready")
        stats_done = sem("stats_done2")
        mv_ready = sem("mv_ready2")
        eps_set = sem("eps_set")
        std_ready = sem("std_ready2")
        rstd_ready = sem("rstd_ready2")
        xn_ready = sem("xn_ready2")
        route = sem("route")
        weights_split = sem("weights_split")
        wparts_ready = sem("wparts_ready")
        scale_psum = sem("scale_psum")
        xs_ready = sem("xs_ready")
        up_psum = sem("up_psum")
        hid_ready = sem("hid_ready")
        hsq_ready = sem("hsq_ready")
        down_psum = sem("down_psum")
        eout_ready = sem("eout_ready")
        added = sem("added")

        UP = [psum[:, m, :] for m in range(NHT)]
        DN = psum[:, 3:5, :]
        DNT = DN.rearrange("p b (t c) -> p (b t) c", c=C)
        SCL = psum[:, 5, :]
        PRE = psum[:, 6:8, :]
        PRET = PRE.rearrange("p b (t c) -> p (b t) c", c=C)
        PRE_STEPS = 6
        ROUTE_STEPS = 9
        block = ctx.enter_context(nc.Block())

        @block.sync
        def _(sp):
            def load(i, p):
                n = 2 * i + p
                sp.dma_start(yb[:, p], y_all[:, bass.ds(n * TPC, TPC), :]).then_inc(y_loaded[p], 16)
                sp.dma_start(xb[:, p], x_ch[bass.ds(n, 1)].rearrange("o p t d -> p (o t) d")
                             ).then_inc(x_loaded[p], 16)

            def store(i, p):
                n = 2 * i + p
                wait_alone(sp, added, SLOTS * (n + 1), sp_passed)
                sp.dma_start(out_ch[bass.ds(n, 1)].rearrange("o p t d -> p (o t) d"), acc[:, p]
                             ).then_inc(out_stored[p], 16)

            load(0, 0)
            for dst, src in ((wov, wov_t), (wou, wou_t), (gate, gate_t), (bias, bias_b), (lower, tri),
                             (pickf, sel)):
                sp.dma_start(dst[:], src).then_inc(small, 16)
            load(0, 1)
            sp.dma_start(swup[:], swup_t).then_inc(big, 16)
            sp.dma_start(swdn[:], swdn_t).then_inc(big, 16)
            def pair(i):
                for p in range(2):
                    wait_alone(sp, pre_ready, PRE_STEPS * (2 * i + p) + 3, sp_passed)
                    load(i + 1, p)
                    store(i, p)

            pair(0)
            with sp.Fori(1, NCHUNK // 2 - 1) as i:
                pair(i)
            for p in range(2):
                store(NCHUNK // 2 - 1, p)
            for p in range(2):
                sp.wait_ge(out_stored[p], 16 * NCHUNK // 2)

        @block.tensor
        def _(pe):
            def pre_start(n, step):
                wait_from_one(pe, pre_ready, PRE_STEPS * n + step)

            def turn_y(i, p):
                n = 2 * i + p
                pre_start(n, 0)
                pe.wait_ge(y_loaded[p], 16 * (i + 1))
                for k in range(KT):
                    for t in range(TPC):
                        last = pe.transpose(PRE[:, k, t * P:(t + 1) * P], yb[:, p, t, k * P:(k + 1) * P],
                                            identf[:])
                last.then_inc(pre_psum, 1)

            def project_down(n):
                pre_start(n, 1)
                for k in range(KT):
                    last = pe.matmul(PRE[0:RANK, 0, :], wov[:, k, :], ybt[:, k, :],
                                     start=k == 0, stop=k == KT - 1)
                last.then_inc(pre_psum, 1)

            def project_up(n):
                pre_start(n, 2)
                for t in range(TPC):
                    last = pe.matmul(PRET[:, t, :], zt[:, t * P:(t + 1) * P], wou[:], start=True, stop=True)
                last.then_inc(pre_psum, 1)

            def turn_x(n):
                pre_start(n, 3)
                pe.wait_ge(xn_ready, n + 1)
                for k in range(KT):
                    for t in range(TPC):
                        last = pe.transpose(PRE[:, k, t * P:(t + 1) * P], xn[:, t, k * P:(k + 1) * P],
                                            identf[:])
                last.then_inc(pre_psum, 1)

            def gate_logits(n, p):
                pre_start(n, 4)
                for t in range(TPC):
                    for k in range(KT):
                        last = pe.matmul(PRE[:, 0, t * E:(t + 1) * E], xnt[:, p, k, t * P:(t + 1) * P],
                                         gate[:, k, :], start=k == 0, stop=k == KT - 1)
                last.then_inc(pre_psum, 1)

            def turn_weights(n):
                pre_start(n, 5)
                pe.wait_ge(wparts_ready, n + 1)
                rows = PRE[0:3 * E, 1, :].bitcast(BF16)
                for t in range(TPC):
                    last = pe.transpose(rows[:, t * P:(t + 1) * P],
                                        wparts[:, t].rearrange("p a e -> p (a e)"), identb[:])
                last.then_inc(pre_psum, 1)

            def spread(n, p, e):
                if e == 0:
                    pe.wait_ge(pre_ready, PRE_STEPS * (n + 1))
                wait_from_one(pe, xs_ready, E * n + e)
                pe.matmul(SCL, pick[:, e, :], wrows[:, p, :], start=True, stop=True).then_inc(scale_psum, 1)

            def up(n, p, s):
                if s < E:
                    pe.wait_ge(xs_ready, E * n + s + 1)
                for m in range(NHT):
                    wait_from_one(pe, hid_ready, NHT * (SLOTS * n + s - 1) + m + 1)
                    for k in range(KT):
                        cols = slice(m * P, m * P + HT[m])
                        w = wup[:, s, k, cols] if s < E else swup[:, k, cols]
                        r = xs[:, s % 2, k, :] if s < E else xnt[:, p, k, :]
                        last = pe.matmul(UP[m][0:HT[m], :], w, r, start=k == 0, stop=k == KT - 1)
                    last.then_inc(up_psum, 1)

            def down(n, s):
                pe.wait_ge(hsq_ready, SLOTS * n + s + 1)
                wait_from_one(pe, eout_ready, SLOTS * n + s)
                for t in range(TPC):
                    for m in range(NHT):
                        h = (hsq[0:HT[m], s % 2, m] if s < E else shsq[0:HT[m], m])[:, t * P:(t + 1) * P]
                        w = wdn[0:HT[m], s, m, :] if s < E else swdn[0:HT[m], m, :]
                        last = pe.matmul(DNT[:, t, :], h, w, start=m == 0, stop=m == NHT - 1)
                last.then_inc(down_psum, 1)

            def chunk(i, p, more=True):
                n = 2 * i + p
                ni, np_ = i + p, 1 - p
                for s in range(SLOTS):
                    if s + 2 < E:
                        spread(n, p, s + 2)
                    elif more and s + 2 >= SLOTS:
                        spread(n + 1, np_, s + 2 - SLOTS)
                    if s + 1 < SLOTS:
                        up(n, p, s + 1)
                    elif more:
                        up(n + 1, np_, 0)
                    if more:
                        if s == 0:
                            turn_y(ni, np_)
                        if s == 1:
                            project_down(n + 1)
                        if s == 2:
                            project_up(n + 1)
                        if s == 4:
                            turn_x(n + 1)
                        if s == 5:
                            gate_logits(n + 1, np_)
                        if s == 6:
                            turn_weights(n + 1)
                    down(n, s)

            pe.wait_ge(small, 6 * 16)
            turn_y(0, 0)
            project_down(0)
            project_up(0)
            turn_x(0)
            gate_logits(0, 0)
            turn_weights(0)
            pe.wait_ge(pick_ready, 1)
            spread(0, 0, 0)
            spread(0, 0, 1)
            pe.wait_ge(cast, 32)
            pe.wait_ge(big, 32)
            up(0, 0, 0)
            chunk(0, 0)
            chunk(0, 1)
            with pe.Fori(1, NCHUNK // 2 - 1) as i:
                chunk(i, 0)
                chunk(i, 1)
            chunk(NCHUNK // 2 - 1, 0)
            chunk(NCHUNK // 2 - 1, 1, more=False)

        @block.scalar
        def _(act):
            def pre_copy(n, step, dst, src):
                act.wait_ge(pre_psum, PRE_STEPS * n + step + 1)
                act.activation(dst, src, ACT.Copy).then_inc(pre_ready, 1)

            def deviation(n):
                act.wait_ge(mv_ready, n + 1)
                act.activation(std[:], mv[:, :, 1], ACT.Sqrt, bias=eps[:]).then_inc(std_ready, 1)

            def gate_exp(n):
                act.wait_ge(pre_psum, PRE_STEPS * n + 5)
                wait_from_one(act, wparts_ready, n)
                act.activation(neg[:], PRE[:, 0, 0:TPC * E].rearrange("p (t e) -> p t e", e=E), ACT.Exp,
                               scale=-1.0).then_inc(pre_ready, 1)

            def relu(n, s):
                u = SLOTS * n + s
                for m in range(NHT):
                    act.wait_ge(up_psum, NHT * u + m + 1)
                    if m == 0:
                        wait_from_one(act, hsq_ready, u - 1)
                    dst = hid[0:HT[m], s % 2, m] if s < E else shid[0:HT[m], m]
                    act.activation(dst, UP[m][0:HT[m], :], ACT.Relu).then_inc(hid_ready, 1)

            def round_out(n, s):
                u = SLOTS * n + s
                act.wait_ge(down_psum, u + 1)
                wait_from_one(act, added, u - 1 if s else u)
                act.activation(eout[:, s % 2] if s < E else sout[:], DNT, ACT.Copy).then_inc(eout_ready, 1)

            def chunk(i, p, more=True):
                n = 2 * i + p
                for s in range(SLOTS):
                    if s + 1 < SLOTS:
                        relu(n, s + 1)
                    elif more:
                        relu(n + 1, 0)
                    if more:
                        if s == 0:
                            pre_copy(n + 1, 0, ybt[:], PRE)
                        if s == 1:
                            pre_copy(n + 1, 1, zt[:], PRE[0:RANK, 0, :])
                        if s == 3:
                            deviation(n + 1)
                        if s == 4:
                            pre_copy(n + 1, 3, xnt[:, 1 - p], PRE)
                        if s == 5:
                            gate_exp(n + 1)
                    round_out(n, s)

            pre_copy(0, 0, ybt[:], PRE)
            pre_copy(0, 1, zt[:], PRE[0:RANK, 0, :])
            act.wait_ge(eps_set, 1)
            deviation(0)
            pre_copy(0, 3, xnt[:, 0], PRE)
            gate_exp(0)
            relu(0, 0)
            chunk(0, 0)
            chunk(0, 1)
            with act.Fori(1, NCHUNK // 2 - 1) as i:
                chunk(i, 0)
                chunk(i, 1)
            chunk(NCHUNK // 2 - 1, 0)
            chunk(NCHUNK // 2 - 1, 1, more=False)

        @block.vector
        def _(dve):
            def residual_norm(i, p):
                n = 2 * i + p
                dve.wait_ge(pre_psum, PRE_STEPS * n + 3)
                dve.wait_ge(x_loaded[p], 16 * (i + 1))
                wait_from_one(dve, out_stored[p], 16 * i)
                dve.tensor_tensor(acc[:, p], xb[:, p], PRET, ALU.add).then_inc(pre_ready, 1)
                dve.wait_ge(pre_ready, PRE_STEPS * n + 3)
                for t in range(TPC):
                    last = dve.bn_stats(stats[:, t, :], acc[:, p, t, :])
                last.then_inc(stats_done, 1)
                wait_alone(dve, stats_done, n + 1, dve_passed)
                for t in range(TPC):
                    last = dve.bn_aggr(mv[:, t, :], stats[:, t, :])
                last.then_inc(mv_ready, 1)

            def normalise(n, p):
                dve.wait_ge(std_ready, n + 1)
                dve.reciprocal(rstd[:], std[:]).then_inc(rstd_ready, 1)
                dve.wait_ge(rstd_ready, n + 1)
                for t in range(TPC):
                    last = dve.tensor_scalar(xn[:, t, :], acc[:, p, t, :], mv[:, t, 0:1],
                                             rstd[:, t:t + 1], ALU.subtract, ALU.mult)
                last.then_inc(xn_ready, 1)

            def routing(n):
                count = [ROUTE_STEPS * n]

                def then(ins):
                    count[0] = count[0] + 1
                    ins.then_inc(route, 1)
                    dve.wait_ge(route, count[0])

                dve.wait_ge(pre_ready, PRE_STEPS * n + 5)
                then(dve.tensor_scalar(neg[:], neg[:], 1.0, None, ALU.add))
                then(dve.reciprocal(score[:], neg[:]))
                then(dve.tensor_tensor(biased[:], score[:],
                                       bias[:].unsqueeze(1).to_broadcast([P, TPC, E]), ALU.add))
                other = biased[:].unsqueeze(2).to_broadcast([P, TPC, E, E])
                own = biased[:].unsqueeze(3).to_broadcast([P, TPC, E, E])
                dve.tensor_tensor(above[:], other, own, ALU.is_gt)
                then(dve.tensor_tensor(equal[:], other, own, ALU.is_equal))
                low = lower[:].rearrange("p (a b) -> p a b", b=E).unsqueeze(1).to_broadcast([P, TPC, E, E])
                then(dve.tensor_tensor(equal[:], equal[:], low, ALU.mult))
                then(dve.tensor_tensor(above[:], above[:], equal[:], ALU.add))
                then(dve.tensor_reduce(rank[:], above[:], AX.X, ALU.add))
                then(dve.scalar_tensor_tensor(out=weight[:], in0=rank[:], scalar=2.0, in1=score[:],
                                              op0=ALU.is_lt, op1=ALU.mult))
                then(dve.tensor_copy(wparts[:, :, 0, :], weight[:]))
                assert ROUTE_STEPS == 9

            def split_weights(n):
                dve.tensor_tensor(wrest[:], weight[:], wparts[:, :, 0, :], ALU.subtract
                                  ).then_inc(weights_split, 1)
                dve.wait_ge(weights_split, 2 * n + 1)
                dve.tensor_copy(wparts[:, :, 1, :], wrest[:]).then_inc(weights_split, 1)
                dve.wait_ge(weights_split, 2 * n + 2)
                dve.tensor_tensor(wparts[:, :, 2, :], wrest[:], wparts[:, :, 1, :], ALU.subtract
                                  ).then_inc(wparts_ready, 1)

            def copy_weights(n, p):
                dve.wait_ge(pre_psum, PRE_STEPS * n + 6)
                dve.tensor_copy(wrows[:, p, :], PRE[0:3 * E, 1, :].bitcast(BF16)[:, 0:CH]
                                ).then_inc(pre_ready, 1)

            def scale_x(n, p, e):
                dve.wait_ge(scale_psum, E * n + e + 1)
                if e > 1:
                    dve.wait_ge(up_psum, NHT * (SLOTS * n + e - 1))
                else:
                    wait_from_one(dve, up_psum, NHT * (SLOTS * (n - 1) + E - 1 + e))
                dve.tensor_tensor(xs[:, e % 2], xnt[:, p], SCL.unsqueeze(1).to_broadcast([P, KT, CH]),
                                  ALU.mult).then_inc(xs_ready, 1)

            def square(n, s):
                u = SLOTS * n + s
                src, dst = (hid[:, s % 2], hsq[:, s % 2]) if s < E else (shid[:], shsq[:])
                dve.wait_ge(hid_ready, NHT * (u + 1))
                wait_from_one(dve, down_psum, u - 1)
                dve.tensor_tensor(dst[:, 0:2], src[:, 0:2], src[:, 0:2], ALU.mult)
                dve.tensor_tensor(dst[0:HT[2], 2], src[0:HT[2], 2], src[0:HT[2], 2], ALU.mult
                                  ).then_inc(hsq_ready, 1)

            def chunk(i, p, more=True):
                n = 2 * i + p
                ni, np_ = i + p, 1 - p
                for s in range(SLOTS):
                    if s + 2 < E:
                        scale_x(n, p, s + 2)
                    elif more and s + 2 >= SLOTS:
                        scale_x(n + 1, np_, s + 2 - SLOTS)
                    if s + 1 < SLOTS:
                        square(n, s + 1)
                    elif more:
                        square(n + 1, 0)
                    if more:
                        if s == 2:
                            residual_norm(ni, np_)
                        if s == 3:
                            normalise(n + 1, np_)
                        if s == 5:
                            routing(n + 1)
                            split_weights(n + 1)
                        if s == 6:
                            copy_weights(n + 1, np_)

            dve.memset(eps[:], EPS).then_inc(eps_set, 1)
            dve.wait_ge(small, 6 * 16)
            dve.tensor_copy(pick[:], pickf[:]).then_inc(pick_ready, 1)
            residual_norm(0, 0)
            normalise(0, 0)
            routing(0)
            split_weights(0)
            copy_weights(0, 0)
            scale_x(0, 0, 0)
            scale_x(0, 0, 1)
            square(0, 0)
            chunk(0, 0)
            chunk(0, 1)
            with dve.Fori(1, NCHUNK // 2 - 1) as i:
                chunk(i, 0)
                chunk(i, 1)
            chunk(NCHUNK // 2 - 1, 0)
            chunk(NCHUNK // 2 - 1, 1, more=False)

        @block.gpsimd
        def _(pool):
            def add_out(n, p, s):
                u = SLOTS * n + s
                pool.wait_ge(eout_ready, u + 1)
                wait_from_one(pool, added, u)
                pool.tensor_tensor(acc[:, p], acc[:, p], eout[:, s % 2] if s < E else sout[:], ALU.add
                                   ).then_inc(added, 1)

            def chunk(i, p, more=True):
                n = 2 * i + p
                for s in range(SLOTS):
                    add_out(n, p, s)

            pool.dma_start(wup[:], wup_t).then_inc(cast, 16)
            pool.dma_start(wdn[:], wdn_t).then_inc(cast, 16)
            chunk(0, 0)
            chunk(0, 1)
            with pool.Fori(1, NCHUNK // 2 - 1) as i:
                chunk(i, 0)
                chunk(i, 1)
            chunk(NCHUNK // 2 - 1, 0)
            chunk(NCHUNK // 2 - 1, 1, more=False)


def kernel(**inputs):
    import numpy as np
    import concourse.bacc as bacc
    from concourse.bass_utils import run_bass_kernel_spmd

    def a(name):
        return np.asarray(inputs[name])

    def by_partition(w):
        k, n = w.shape
        tiles = -(-k // P)
        full = np.zeros((tiles * P, n), w.dtype)
        full[:k] = w
        return full.reshape(tiles, P, n).transpose(1, 0, 2)

    experts = range(E)
    eye3 = np.zeros((3, E, E, P), np.float32)
    for e in experts:
        eye3[:, e, e, :] = 1.0
    arrays = {
        "x": a("L0_attn_x"),
        "wv_t": by_partition(a("L0_attn_W_qkv_v").T),
        "wu_t": a("L0_attn_W_qkv_u").T,
        "wov_t": by_partition(a("L0_attn_W_o_v").T),
        "wou_t": a("L0_attn_W_o_u").T,
        "gate_t": by_partition(a("L0_ffn_gate_w").T),
        "bias_b": np.tile(a("L0_ffn_expert_bias")[None, :], (P, 1)),
        "wup_t": np.stack([by_partition(a("L0_ffn_w_up")[e].T) for e in experts], 1),
        "wdn_t": np.stack([by_partition(a("L0_ffn_w_down")[e].T) for e in experts], 1),
        "swup_t": by_partition(a("L0_ffn_shared_w_up").T),
        "swdn_t": by_partition(a("L0_ffn_shared_w_down").T),
        "ident": np.eye(P, dtype=np.float32),
        "tri": np.tile(np.tril(np.ones((E, E), np.float32), -1).reshape(1, E * E), (P, 1)),
        "sel": eye3.reshape(3 * E, E, P),
    }
    arrays = {k: np.ascontiguousarray(v) for k, v in arrays.items()}
    nc = bacc.Bacc("TRN2", target_bir_lowering=False, num_devices=1)
    args = [nc.dram_tensor(k, v.shape, mybir.dt.from_np(v.dtype), kind="ExternalInput").ap()
            for k, v in arrays.items()]
    args.append(nc.dram_tensor("out", (B, T, C), F32, kind="ExternalOutput").ap())
    build(nc, *args)
    r = run_bass_kernel_spmd(nc, [arrays], core_ids=[0])
    return r.results[0]["out"]
```

```python
from contextlib import ExitStack

import concourse.bass as bass
from concourse import mybir

P = 128
B, T, C = 2, 2048, 256
NH, HD = 16, 16
RANK = 64
E, HID = 8, 352
EPS = 1e-5
SCALE = HD ** -0.5

CH = 512
TPC = CH // P
KT = C // P
NCHUNK = B * T // CH
HG = 4
NG = B * NH // HG
QPG = T // CH
UNITS = NG * QPG
ST = T // P
NPROD = 6
KROWS = NPROD * HD
QPART = (0, 0, 0, 1, 1, 2)
KPART = (0, 1, 2, 0, 1, 0)
ROWS = KROWS + 3
VW = HD + 1
HT = [P, P, HID - 2 * P]
NHT = len(HT)
SLOTS = E + 1
EP = 32

ALU = mybir.AluOpType
ACT = mybir.ActivationFunctionType
AX = mybir.AxisListType
F32 = mybir.dt.float32
BF16 = mybir.dt.bfloat16


def wait_from_one(eng, sem, value):
    if not isinstance(value, int) or value > 0:
        eng.wait_ge(sem, value)


def wait_alone(eng, sem, value, passed):
    eng.wait_ge(sem, value)
    if not isinstance(value, int):
        eng.sem_inc(passed, 1)


def build(nc, x, wv_t, wu_t, wov_t, wou_t, gate_t, bias_b, wup_t, wdn_t, swup_t, swdn_t,
          ident, tri, sel, out):
    parts_d = nc.dram_tensor("parts_d", [3, 2 * C, B * T], BF16).ap()
    v_d = nc.dram_tensor("v_d", [B, P, ST, NH * VW], F32).ap()
    x_ch = x.rearrange("b (c t p) d -> (b c) p t d", p=P, t=TPC)
    out_ch = out.rearrange("b (c t p) d -> (b c) p t d", p=P, t=TPC)

    with ExitStack() as ctx:
        psum = ctx.enter_context(nc.psum_tensor("psum", [P, 8, CH], F32))
        identf = ctx.enter_context(nc.sbuf_tensor("identf", [P, P], F32))
        identb = ctx.enter_context(nc.sbuf_tensor("identb", [P, P], BF16))
        y_all = ctx.enter_context(nc.sbuf_tensor("y_all", [P, B * T // P, C], F32))
        vcur = ctx.enter_context(nc.sbuf_tensor("vcur", [P, ST, HG, VW], F32))
        stacks_loaded = ctx.enter_context(nc.semaphore("stacks_loaded"))
        v_loaded = ctx.enter_context(nc.semaphore("v_loaded"))
        rest_ready = ctx.enter_context(nc.semaphore("rest_ready"))
        v_ready = ctx.enter_context(nc.semaphore("v_ready"))
        ring_used = ctx.enter_context(nc.semaphore("ring_used"))
        pv_done = ctx.enter_context(nc.semaphore("pv_done"))

        with ExitStack() as right:
            kst = right.enter_context(nc.sbuf_tensor("kst", [ROWS, HG, 2 * T], BF16, side="right"))
            qst = right.enter_context(nc.sbuf_tensor("qst", [ROWS, HG, 2 * T], BF16, side="right"))

            def load_stacks(sp, g, sides=(0, 1)):
                batch, row = g // (NH // HG), (g % (NH // HG)) * HG * HD
                for side in sides:
                    stack, part = ((qst, QPART), (kst, KPART))[side]
                    for j in range(NPROD):
                        src = parts_d[part[j], bass.ds(side * C + row, HG * HD), bass.ds(batch * T, T)]
                        sp.dma_start(stack[j * HD:(j + 1) * HD, :, bass.ds((g % 2) * T, T)],
                                     src.rearrange("(h d) t -> d h t", d=HD)
                                     ).then_inc(stacks_loaded, 16)

            def load_v(sp, g, q):
                batch, col = g // (NH // HG), (g % (NH // HG)) * HG * VW
                sp.dma_start(vcur[:, q * 4:(q + 1) * 4].rearrange("p s h c -> p s (h c)"),
                             v_d[bass.ds(batch, 1), :, q * 4:(q + 1) * 4, bass.ds(col, HG * VW)]
                             .rearrange("o p s c -> p (o s) c")).then_inc(v_loaded, 16)

            attend = attention_units(nc, ctx, psum, identf, identb, y_all, kst, qst, vcur,
                                     stacks_loaded, v_loaded, rest_ready, v_ready, ring_used, pv_done,
                                     load_stacks, load_v)
            with ExitStack() as left:
                project = project_qkv(nc, ctx, left, psum, identf, identb, y_all, x_ch, wv_t, wu_t, ident,
                                      parts_d, v_d, kst, load_stacks, load_v, v_loaded, rest_ready,
                                      v_ready)
        experts = mix_experts(nc, ctx, psum, identf, identb, y_all, x_ch, out_ch, wov_t, wou_t, gate_t,
                              bias_b, wup_t, wdn_t, swup_t, swdn_t, tri, sel, ring_used, pv_done,
                              attend["output_placed"])
        run_engines(nc, project, attend, experts)


def run_engines(nc, project, attend, experts):
    with nc.Block() as block:
        @block.sync
        def _(sp):
            ahead, rest = experts["sync"](sp)
            project["sync"](sp)
            attend["sync"](sp, ahead)
            rest()

        @block.tensor
        def _(pe):
            ahead, rest = experts["tensor"](pe)
            project["tensor"](pe)
            attend["tensor"](pe, ahead)
            rest()

        @block.scalar
        def _(act):
            ahead, rest = experts["scalar"](act)
            project["scalar"](act)
            attend["scalar"](act, ahead)
            rest()

        @block.vector
        def _(dve):
            ahead, rest = experts["vector"](dve)
            project["vector"](dve)
            attend["vector"](dve, ahead)
            rest()

        @block.gpsimd
        def _(pool):
            ahead, rest = experts["gpsimd"](pool)
            project["gpsimd"](pool)
            attend["gpsimd"](pool, ahead)
            rest()


def project_qkv(nc, ctx, mem, psum, identf, identb, y_all, x_ch, wv_t, wu_t, ident, parts_d, v_d, kst,
                load_stacks, load_v, v_loaded, rest_ready, v_ready):
    def sb(name, shape, dt=F32):
        return mem.enter_context(nc.sbuf_tensor(name, shape, dt, side="left"))

    def sem(name):
        return ctx.enter_context(nc.semaphore(name))

    wv = sb("wv", [P, KT, RANK])
    wu = sb("wu", [P, 3 * C])
    xin = y_all[:].rearrange("p (c t) d -> p c t d", t=TPC)
    stats = sb("stats", [P, TPC, 6])
    mv = sb("mv", [P, TPC, 2])
    eps = sb("eps", [P, 1])
    std = sb("std", [P, TPC])
    rstd = sb("rstd", [P, TPC])
    xn = sb("xn", [P, 2, TPC, C])
    xnt = sb("xnt", [P, KT, CH])
    at = sb("at", [P, CH])
    parts = sb("parts", [P, 2, 3, 2 * KT, CH], BF16)
    rest = sb("rest", [P, 2, 2 * KT, CH])
    vst = sb("vst", [P, 2, TPC, NH, VW])

    sp_passed = sem("sp_passed")
    dve_passed = sem("dve_passed")
    weights = sem("weights")
    eps_set = sem("eps_set0")
    consts = sem("consts")
    warm = sb("warm", [P, 1])
    ones_set = sem("ones_set")
    x_loaded = [sem(f"x_loaded{j}") for j in range(4)]
    stats_done = sem("stats_done")
    mv_ready = sem("mv_ready")
    std_ready = sem("std_ready")
    rstd_ready = sem("rstd_ready")
    xn_ready = sem("xn_ready")
    xt_psum = sem("xt_psum")
    xt_ready = sem("xt_ready")
    at_psum = sem("at_psum")
    at_ready = sem("at_ready")
    qk_psum = sem("qk_psum")
    v_psum = sem("v_psum")
    part0_ready = sem("part0_ready")
    part1_ready = sem("part1_ready")
    part2_ready = sem("part2_ready")
    parts_stored = [sem("parts_stored0"), sem("parts_stored1")]
    v_stored = [sem("v_stored0"), sem("v_stored1")]

    XT, AT, QK, VB = psum[:, 0:2, :], psum[0:RANK, 0, :], psum[:, 3:7, :], (psum[:, 7, :], psum[:, 2, :])

    def sync(sp):
        def load(first, end, loaded):
            sp.dma_start(xin[:, first:end].rearrange("p c t d -> p (c t) d"),
                         x_ch[first:end].rearrange("c p t d -> p c t d")).then_inc(loaded, 16)

        def store(i, p):
            n = 2 * i + p
            for j, ready in enumerate((part0_ready, part1_ready, part2_ready)):
                wait_alone(sp, ready, n + 1, sp_passed)
                sp.dma_start(parts_d[j, :, bass.ds(n * CH, CH)].rearrange("(m p) t -> p m t", p=P),
                             parts[:, p, j]).then_inc(parts_stored[p], 16)
                if j == 0:
                    store_v(i, p)

        def store_v(i, p):
            n = 2 * i + p
            wait_alone(sp, v_ready, n + 1, sp_passed)
            sp.dma_start(v_d[bass.ds(n // QPG, 1), :, bass.ds((n % QPG) * TPC, TPC), :]
                         .rearrange("o p t c -> p (o t) c"),
                         vst[:, p].rearrange("p t h c -> p t (h c)")).then_inc(v_stored[p], 16)

        load(0, 1, x_loaded[0])
        sp.dma_start(identf[:], ident).then_inc(weights, 16)
        sp.dma_start(wv[:], wv_t).then_inc(weights, 16)
        sp.dma_start(wu[0:RANK], wu_t).then_inc(weights, 16)
        load(1, 2, x_loaded[1])
        load(2, 4, x_loaded[2])
        load(4, NCHUNK, x_loaded[3])

        half = NCHUNK // B // 2
        for i in range(NCHUNK // 2):
            if i == half:
                for p in range(2):
                    sp.wait_ge(parts_stored[p], 3 * 16 * half)
                    sp.wait_ge(v_stored[p], 16 * half)
            for p in range(2):
                store(i, p)
                if i == half:
                    load_stacks(sp, 0, (p,))
                if i >= half:
                    q = 2 * (i - half) + p
                    wait_from_one(sp, v_loaded, 16 * q)
                    load_v(sp, 0, q)
        sp.wait_ge(v_loaded, 16 * 4)
        for p in range(2):
            wait_alone(sp, parts_stored[p], 3 * 16 * NCHUNK // 2, sp_passed)
            wait_alone(sp, v_stored[p], 16 * NCHUNK // 2, sp_passed)

    def vector(dve):
        def statistics(i, p):
            n = 2 * i + p
            if isinstance(i, int) and i < 2:
                dve.wait_ge(x_loaded[2 * i + (p if i == 0 else 0)], 16)
            else:
                dve.wait_ge(x_loaded[3], 16)
            wait_from_one(dve, xn_ready, n)
            for t in range(TPC):
                last = dve.bn_stats(stats[:, t, :], y_all[:, bass.ds(n * TPC + t, 1), :]
                                    .rearrange("p o d -> p (o d)"))
            last.then_inc(stats_done, 1)
            wait_alone(dve, stats_done, n + 1, dve_passed)
            for t in range(TPC):
                last = dve.bn_aggr(mv[:, t, :], stats[:, t, :])
            last.then_inc(mv_ready, 1)

        def normalise(i, p):
            n = 2 * i + p
            dve.wait_ge(std_ready, n + 1)
            dve.reciprocal(rstd[:], std[:]).then_inc(rstd_ready, 1)
            dve.wait_ge(rstd_ready, n + 1)
            wait_from_one(dve, xt_psum, n - 1)
            for t in range(TPC):
                last = dve.tensor_scalar(xn[:, p, t, :], y_all[:, bass.ds(n * TPC + t, 1), :]
                                         .rearrange("p o d -> p (o d)"), mv[:, t, 0:1],
                                         rstd[:, t:t + 1], ALU.subtract, ALU.mult)
            last.then_inc(xn_ready, 1)

        def take_rest(i, p):
            n = 2 * i + p
            dve.wait_ge(part0_ready, n + 1)
            wait_from_one(dve, part2_ready, n - 1)
            dve.tensor_tensor(rest[:, p], QK, parts[:, p, 0], ALU.subtract).then_inc(rest_ready, 1)

        dve.memset(eps[:], EPS).then_inc(eps_set, 1)
        dve.memset(at[RANK:P], 0.0)
        dve.memset(wu[RANK:P], 0.0)
        dve.memset(vst[:, 0, :, :, HD:VW], 1.0)
        dve.memset(vst[:, 1, :, :, HD:VW], 1.0).then_inc(consts, 1)
        for p in range(2):
            statistics(0, p)
            normalise(0, p)
        dve.wait_ge(weights, 48)
        dve.tensor_copy(identb[:], identf[:]).then_inc(consts, 1)

        def pair(i):
            for p in range(2):
                statistics(i + 1, p)
                normalise(i + 1, p)
                take_rest(i, p)

        pair(0)
        with dve.Fori(1, NCHUNK // 2 - 1) as i:
            pair(i)
        take_rest(NCHUNK // 2 - 1, 0)
        take_rest(NCHUNK // 2 - 1, 1)

    def gpsimd(pool):
        def last_part(i, p):
            n = 2 * i + p
            pool.wait_ge(part1_ready, n + 1)
            pool.tensor_tensor(parts[:, p, 2], rest[:, p], parts[:, p, 1], ALU.subtract
                               ).then_inc(part2_ready, 1)

        pool.memset(kst[KROWS:ROWS], 1.0).then_inc(ones_set, 1)
        pool.wait_ge(ones_set, 1)
        last_part(0, 0)
        with pool.Fori(1, NCHUNK // 2) as i:
            last_part(i - 1, 1)
            last_part(i, 0)
        last_part(NCHUNK // 2 - 1, 1)

    def tensor(pe):
        def transpose_x(i, p):
            n = 2 * i + p
            pe.wait_ge(xn_ready, n + 1)
            wait_from_one(pe, xt_ready, n)
            for k in reversed(range(KT)):
                if k == 0:
                    wait_from_one(pe, at_ready, n)
                for t in range(TPC):
                    last = pe.transpose(XT[:, k, t * P:(t + 1) * P],
                                        xn[:, p, t, k * P:(k + 1) * P], identf[:])
            last.then_inc(xt_psum, 1)

        def project_down(n):
            pe.wait_ge(xt_ready, n + 1)
            for k in range(KT):
                last = pe.matmul(AT, wv[:, k, :], xnt[:, k, :], start=k == 0, stop=k == KT - 1)
            last.then_inc(at_psum, 1)

        def project_up(n):
            pe.wait_ge(at_ready, n + 1)
            wait_from_one(pe, rest_ready, n)
            for m in range(2 * KT):
                last = pe.matmul(QK[:, m, :], wu[:, m * P:(m + 1) * P], at[:], start=True, stop=True)
            last.then_inc(qk_psum, 1)
            wait_from_one(pe, v_ready, n)
            for t in range(TPC):
                last = pe.matmul(VB[t // 2][:, (t % 2) * C:(t % 2 + 1) * C], at[:, t * P:(t + 1) * P],
                                 wu[:, 2 * C:3 * C], start=True, stop=True)
            last.then_inc(v_psum, 1)

        pe.wait_ge(weights, 48)
        pe.wait_ge(consts, 1)
        def pair(i):
            for p in range(2):
                project_down(2 * i + p)
                transpose_x(i + p, 1 - p)
                project_up(2 * i + p)

        transpose_x(0, 0)
        pair(0)
        with pe.Fori(1, NCHUNK // 2 - 1) as i:
            pair(i)
        i = NCHUNK // 2 - 1
        project_down(2 * i)
        transpose_x(i, 1)
        project_up(2 * i)
        project_down(2 * i + 1)
        project_up(2 * i + 1)

    def scalar(act):
        def deviation(n):
            act.wait_ge(mv_ready, n + 1)
            act.activation(std[:], mv[:, :, 1], ACT.Sqrt, bias=eps[:]).then_inc(std_ready, 1)

        def copy_xt(n):
            act.wait_ge(xt_psum, n + 1)
            wait_from_one(act, at_psum, n)
            act.activation(xnt[:], XT, ACT.Copy).then_inc(xt_ready, 1)

        def copy_at(n):
            act.wait_ge(at_psum, n + 1)
            wait_from_one(act, v_psum, n)
            act.activation(at[0:RANK], AT, ACT.Copy).then_inc(at_ready, 1)

        def copy_qkv(i, p, more=True):
            n = 2 * i + p
            if more:
                deviation(n + 2)
            act.wait_ge(qk_psum, n + 1)
            wait_from_one(act, parts_stored[p], 48 * i)
            act.activation(parts[:, p, 0], QK, ACT.Copy).then_inc(part0_ready, 1)
            act.wait_ge(v_psum, n + 1)
            wait_from_one(act, v_stored[p], 16 * i)
            for j in range(2):
                last = act.activation(vst[:, p, 2 * j:2 * j + 2, :, 0:HD],
                                      VB[j].rearrange("p (t h c) -> p t h c", t=2, h=NH), ACT.Copy)
            last.then_inc(v_ready, 1)

        def middle_part(i, p):
            act.wait_ge(rest_ready, 2 * i + p + 1)
            act.activation(parts[:, p, 1], rest[:, p], ACT.Copy).then_inc(part1_ready, 1)

        act.wait_ge(eps_set, 1)
        act.activation(warm[:], eps[:], ACT.Sqrt)
        act.wait_ge(consts, 1)
        deviation(0)
        copy_xt(0)
        deviation(1)

        def pair(i):
            for p in range(2):
                copy_at(2 * i + p)
                copy_xt(2 * i + p + 1)
                if p == 1 or not isinstance(i, int) or i > 0:
                    middle_part(i - 1 + p, 1 - p)
                copy_qkv(i, p)

        pair(0)
        with act.Fori(1, NCHUNK // 2 - 1) as i:
            pair(i)
        i = NCHUNK // 2 - 1
        copy_at(2 * i)
        copy_xt(2 * i + 1)
        middle_part(i - 1, 1)
        copy_qkv(i, 0, more=False)
        copy_at(2 * i + 1)
        middle_part(i, 0)
        copy_qkv(i, 1, more=False)
        middle_part(i, 1)

    return {"sync": sync, "tensor": tensor, "scalar": scalar, "vector": vector, "gpsimd": gpsimd}


def attention_units(nc, ctx, psum, identf, identb, y_all, kst, qst, vcur, stacks_loaded, v_loaded,
                    rest_ready, v_ready, ring_used, pv_done, load_stacks, load_v):
    def sb(name, shape, dt=F32):
        return ctx.enter_context(nc.sbuf_tensor(name, shape, dt))

    def sem(name):
        return ctx.enter_context(nc.semaphore(name))

    PS = 4
    probs = sb("probs", [P, PS, HG, CH])
    SC = T // CH
    mx = sb("mx", [P, 2, HG, SC])
    negmax = sb("negmax", [P, 2, HG])
    mrest = sb("mrest", [P, 2, HG])
    mparts = sb("mparts", [P, 2, 3, HG], BF16)
    mrows = sb("mrows", [3 * HG, 2, P], BF16)
    yt = sb("yt", [P, CH])
    rsum = sb("rsum", [P, TPC, HG])

    sp_passed = sem("sp_passed1")
    pool_passed = sem("pool_passed1")
    acc_zero = sem("acc_zero")
    ring_filled = sem("ring_filled")
    negmax_ready = sem("negmax_ready")
    split_done = sem("split_done")
    mparts_ready = sem("mparts_ready")
    mrows_placed = sem("mrows_placed")
    scores_ready = sem("scores_ready")
    probs_ready = sem("probs_ready")
    yt_ready = sem("yt_ready")
    rsum_ready = sem("rsum_ready")

    SB = [psum[:, h, :] for h in range(HG)]
    ACC = psum[:, 4, :]
    RB = [psum[:, 5 + b, :] for b in range(3)]
    SCORES, MAXIMA, OUTPUTS = range(3)

    def ring_plan(first=False, tiles=TPC, last=False):
        plan = []
        for j in range(ST):
            step = []
            if j % 4 == 1 and j // 4 <= tiles and not last:
                step.append(MAXIMA)
            if j == 3 and not first:
                step.append(OUTPUTS)
            if j // 4 < tiles:
                step += [SCORES] * SC
            plan.append(step)
        return plan

    PER_UNIT = sum(map(len, ring_plan()))
    AHEAD = (TPC + 1) * HG * SC + TPC
    TURN_AFTER = 1
    FIRST = sum(map(len, ring_plan(first=True)))
    assert PER_UNIT % 3 == 0

    def ring_base(u):
        if isinstance(u, int) and u == 0:
            return AHEAD
        if isinstance(u, int) and u == UNITS - 1:
            return ring_base(u - 1) + sum(map(len, ring_plan(tiles=TPC - 1)))
        return AHEAD + FIRST + PER_UNIT * (u - 1)

    def ring_place(j, what, **kind):
        plan = ring_plan(**kind)
        return sum(map(len, plan[:j])) + plan[j].index(what)

    BEFORE_LAST = sum(map(len, ring_plan(tiles=TPC - 1)))
    RING_ENTRIES = ring_base(UNITS - 2) + BEFORE_LAST + 2
    STACK_DMAS = 2 * NPROD
    QT = T // P
    NQ = UNITS * TPC


    def output_placed(u):
        return RING_ENTRIES if u == UNITS - 1 else ring_base(u + 1) + ring_place(3, OUTPUTS) + 1

    def sync(sp, ahead):
        def next_v(g):
            for q in range(4):
                wait_alone(sp, pv_done, (QPG * g - 1) * ST + 4 * q + 4, sp_passed)
                wait_alone(sp, v_loaded, 16 * (4 * g + q), sp_passed)
                load_v(sp, g, q)

        sp.wait_ge(stacks_loaded, 16 * STACK_DMAS)
        load_stacks(sp, 1)
        ahead()
        with sp.Fori(1, NG - 1) as g:
            next_v(g)
            wait_alone(sp, scores_ready, HG * ST * QPG * g, sp_passed)
            wait_alone(sp, stacks_loaded, 16 * STACK_DMAS * (g + 1), sp_passed)
            load_stacks(sp, g + 1)
        next_v(NG - 1)

    def tensor(pe, ahead):
        def score_max(q, h, c, bank, entry):
            wait_from_one(pe, ring_used, entry - 2)
            col = (q % (2 * QT)) * P
            kcol = ((q // QT) % 2) * T + c * CH
            pe.matmul(bank, qst[0:KROWS, h, bass.ds(col, P)], kst[0:KROWS, h, bass.ds(kcol, CH)],
                      start=True, stop=True).then_inc(ring_filled, 1)

        def stack_wait(q):
            pe.wait_ge(stacks_loaded, 16 * STACK_DMAS * (q // QT + 1))

        def turn_maxima(q, par, bank, entry):
            pe.wait_ge(mparts_ready, q + 1)
            pe.wait_ge(ring_used, entry - 2)
            pe.transpose(bank.bitcast(BF16)[0:3 * HG, 0:P], mparts[:, par].rearrange("p a h -> p (a h)"),
                         identb[:]).then_inc(ring_filled, 1)

        def score(u, j, h):
            n = (u * ST + j) * HG + h
            wait_from_one(pe, probs_ready, n - HG + 1)
            qcol = (u % (2 * QPG)) * CH
            kcol = ((u // QPG) % 2) * T + j * P
            pe.matmul(SB[h], kst[:, h, bass.ds(kcol, P)], qst[:, h, bass.ds(qcol, CH)],
                      start=True, stop=True).then_inc(scores_ready, 1)

        def weigh(u, j):
            pe.wait_ge(probs_ready, (u * ST + j + 1) * HG)
            if j % 4 == 0:
                pe.wait_ge(v_loaded, 16 * (4 * (u // QPG) + j // 4 + 1))
            if j == 0:
                wait_from_one(pe, yt_ready, u)
            for h in range(HG):
                last = pe.matmul(ACC[32 * h:32 * h + VW, :], vcur[:, j, h, :], probs[:, j % PS, h, :],
                                 start=j == 0, stop=j == ST - 1)
            last.then_inc(pv_done, 1)

        def turn_y(u, bank, entry, last=False):
            pe.wait_ge(yt_ready, u + 1)
            pe.wait_ge(ring_used, entry if last else entry - 2)
            for t in range(TPC):
                last = pe.transpose(bank[:, t * P:(t + 1) * P], yt[:, t * P:(t + 1) * P], identf[:])
            last.then_inc(ring_filled, 1)

        def unit(u, place, **kind):
            r = 0
            last = kind.get("last", False)
            base = ring_base(u)
            if last:
                pe.wait_ge(ring_used, base)
            for j, step in enumerate(ring_plan(**kind)):
                q = TPC * (u + 1) + 1 + j // 4
                if j % 4 == 0 and SCORES in step:
                    stack_wait(q)
                if j == ST - 1 and not last:
                    pe.wait_ge(mrows_placed, 16 * TPC * (u + 2))
                if MAXIMA in step:
                    turn_maxima(q - 1, (j // 4) % 2, RB[(place + r) % 3], base + r)
                    r += 1
                if OUTPUTS in step:
                    turn_y(u - 1, RB[0] if last else RB[(place + r) % 3], base + r, last)
                    r += 1
                if last:
                    ahead(j)
                for h in range(HG):
                    if j < ST - 1:
                        score(u, j + 1, h)
                    elif not last:
                        score(u + 1, 0, h)
                    if SCORES in step:
                        score_max(q, j % 4, h, RB[(place + r) % 3], base + r)
                        r += 1
                weigh(u, j)

        pe.wait_ge(rest_ready, NCHUNK)
        pe.wait_ge(v_ready, NCHUNK)
        stack_wait(0)
        r = 0
        for q in range(TPC + 1):
            for h in range(HG):
                for c in range(SC):
                    score_max(q, h, c, RB[r % 3], r)
                    r += 1
                if q > 0 and h == TURN_AFTER:
                    turn_maxima(q - 1, (q - 1) % 2, RB[r % 3], r)
                    r += 1
        pe.wait_ge(mrows_placed, 16 * TPC)
        for h in range(HG):
            score(0, 0, h)
        pe.wait_ge(acc_zero, 1)
        unit(0, AHEAD, first=True)
        with pe.Fori(1, UNITS - 2) as u:
            unit(u, AHEAD + FIRST)
        unit(UNITS - 2, ring_base(UNITS - 2), tiles=TPC - 1)
        unit(UNITS - 1, ring_base(UNITS - 2) + BEFORE_LAST, tiles=0, last=True)
        pe.wait_ge(ring_used, RING_ENTRIES - 1)
        ahead(ST)
        turn_y(UNITS - 1, RB[1], RING_ENTRIES - 1, last=True)

    def scalar(act, ahead):
        def exponentials(u, j):
            for h in range(HG):
                n = (u * ST + j) * HG + h
                act.wait_ge(scores_ready, n + 1)
                if h == 0:
                    wait_from_one(act, pv_done, u * ST + j - PS + 1)
                act.activation(probs[:, j % PS, h, :], SB[h], ACT.Exp, scale=SCALE
                               ).then_inc(probs_ready, 1)

        def copy_sums(u, last=False):
            act.wait_ge(pv_done, (u + 1) * ST)
            if not isinstance(u, int) or u > 0:
                kind = {"tiles": 0, "last": True} if last else {}
                act.wait_ge(ring_filled, ring_base(u) + ring_place(3, OUTPUTS, **kind) + 1)
            act.activation(yt[:], ACC, ACT.Copy).then_inc(yt_ready, 1)

        def unit(u, last=False):
            for j in range(ST - 1):
                exponentials(u, j + 1)
                if last:
                    ahead(j)
            if not last:
                exponentials(u + 1, 0)
            copy_sums(u, last)

        exponentials(0, 0)
        unit(0)
        with act.Fori(1, UNITS - 1) as u:
            unit(u)
        unit(UNITS - 1, last=True)

    def vector(dve, ahead):
        def reduce_scores(q, par, h, c, bank, entry):
            dve.wait_ge(ring_filled, entry + 1)
            dve.tensor_reduce(mx[:, par, h, c:c + 1], bank, AX.X, ALU.max).then_inc(ring_used, 1)

        def finish_maxima(q, par, entries):
            dve.wait_ge(ring_used, entries)
            wait_from_one(dve, mparts_ready, q - 1)
            dve.tensor_reduce(negmax[:, par, :], mx[:, par], AX.X, ALU.max, negate=True
                              ).then_inc(negmax_ready, 1)

        def copy_maxima(q, par, bank, entry):
            dve.wait_ge(ring_filled, entry + 1)
            wait_from_one(dve, mrows_placed, 16 * (q - 1))
            dve.tensor_copy(mrows[:, par, :], bank.bitcast(BF16)[0:3 * HG, 0:P]).then_inc(ring_used, 1)

        def divide(u, bank, entry):
            dve.wait_ge(ring_used, entry)
            dve.wait_ge(ring_filled, entry + 1)
            heads = bank.rearrange("p (t h c) -> p t h c", t=TPC, h=HG)
            dve.reciprocal(rsum[:], heads[:, :, :, HD]).then_inc(rsum_ready, 1)
            dve.wait_ge(rsum_ready, u + 1)
            batch, group, chunk = u // (UNITS // B), (u // QPG) % (NH // HG), u % QPG
            tile = batch * (T // P) + chunk * TPC
            dst = y_all[:, bass.ds(tile, TPC), bass.ds(group * (HG * HD), HG * HD)]
            dve.tensor_tensor(dst.rearrange("p t (h c) -> p t h c", h=HG), heads[:, :, :, 0:HD],
                              rsum[:].unsqueeze(3).to_broadcast([P, TPC, HG, HD]), ALU.mult
                              ).then_inc(ring_used, 1)

        def unit(u, place, **kind):
            r = 0
            base = ring_base(u)
            last = kind.get("last", False)
            for j, step in enumerate(ring_plan(**kind)):
                q = TPC * (u + 1) + 1 + j // 4
                par = (1 + j // 4) % 2
                if last:
                    ahead(j)
                if MAXIMA in step:
                    copy_maxima(q - 1, 1 - par, RB[(place + r) % 3], base + r)
                    r += 1
                if OUTPUTS in step:
                    divide(u - 1, RB[0] if last else RB[(place + r) % 3], base + r)
                    r += 1
                if SCORES in step:
                    for c in range(SC):
                        reduce_scores(q, par, j % 4, c, RB[(place + r) % 3], base + r)
                        r += 1
                    if j % 4 == 3:
                        finish_maxima(q, par, base + r)

        dve.wait_ge(rest_ready, NCHUNK)
        dve.memset(ACC, 0.0).then_inc(acc_zero, 1)
        r = 0
        for q in range(TPC + 1):
            for h in range(HG):
                for c in range(SC):
                    reduce_scores(q, q % 2, h, c, RB[r % 3], r)
                    r += 1
                if q > 0 and h == TURN_AFTER:
                    copy_maxima(q - 1, (q - 1) % 2, RB[r % 3], r)
                    r += 1
            finish_maxima(q, q % 2, r)
        unit(0, AHEAD, first=True)
        with dve.Fori(1, UNITS - 2) as u:
            unit(u, AHEAD + FIRST)
        unit(UNITS - 2, ring_base(UNITS - 2), tiles=TPC - 1)
        unit(UNITS - 1, ring_base(UNITS - 2) + BEFORE_LAST, tiles=0, last=True)
        ahead(ST)
        divide(UNITS - 1, RB[1], RING_ENTRIES - 1)

    def gpsimd(pool, ahead):
        def split(q, par, entry):
            wait_alone(pool, negmax_ready, q + 1, pool_passed)
            pool.tensor_copy(mparts[:, par, 0], negmax[:, par]).then_inc(split_done, 1)
            wait_alone(pool, split_done, 3 * q + 1, pool_passed)
            pool.tensor_tensor(mrest[:, par], negmax[:, par], mparts[:, par, 0], ALU.subtract
                               ).then_inc(split_done, 1)
            wait_alone(pool, split_done, 3 * q + 2, pool_passed)
            pool.tensor_copy(mparts[:, par, 1], mrest[:, par]).then_inc(split_done, 1)
            wait_alone(pool, split_done, 3 * q + 3, pool_passed)
            pool.tensor_tensor(mparts[:, par, 2], mrest[:, par], mparts[:, par, 1], ALU.subtract
                               ).then_inc(mparts_ready, 1)
            pool.wait_ge(ring_used, entry + 1)
            wait_from_one(pool, mrows_placed, 16 * q)
            pool.dma_start(qst[KROWS:ROWS, :, bass.ds((q % (2 * QT)) * P, P)],
                           mrows[:, par, :]).then_inc(mrows_placed, 16)

        def unit(u, **kind):
            for i in range(TPC):
                split(TPC * (u + 1) + i, i % 2, ring_base(u) + ring_place(4 * i + 1, MAXIMA, **kind))

        for q in range(TPC):
            split(q, q % 2, HG * SC * (q + 1) + SC * (TURN_AFTER + 1) + q)
        ahead()
        unit(0, first=True)
        with pool.Fori(1, UNITS - 2) as u:
            unit(u)
        unit(UNITS - 2, tiles=TPC - 1)
        pool.wait_ge(mrows_placed, 16 * NQ)

    return {"sync": sync, "tensor": tensor, "scalar": scalar, "vector": vector, "gpsimd": gpsimd,
            "output_placed": output_placed}


def mix_experts(nc, ctx, psum, identf, identb, y_all, x_ch, out_ch, wov_t, wou_t, gate_t, bias_b,
                wup_t, wdn_t, swup_t, swdn_t, tri, sel, ring_used, pv_done, output_placed):
    def sb(name, shape, dt=F32, side="left"):
        return ctx.enter_context(nc.sbuf_tensor(name, shape, dt, side=side))

    def sem(name):
        return ctx.enter_context(nc.semaphore(name))

    wov = sb("wov", [P, KT, RANK])
    wou = sb("wou", [RANK, C])
    gate = sb("gate", [P, KT, EP])
    logits = sb("logits", [TPC * EP, P])
    bias = sb("bias", [P, E])
    lower = sb("lower", [P, E * E])
    pick = sb("pick", [3 * E, E, P], BF16)
    wup = sb("wup", [P, E, KT, HID], BF16)
    wdn = sb("wdn", [P, E, NHT, C], BF16)
    swup = sb("swup", [P, KT, HID], side="right")
    swdn = sb("swdn", [P, NHT, C], side="right")

    yb = sb("yb", [P, 2, TPC, C])
    xb = [sb("xb0", [P, TPC, C]), sb("xb1", [P, TPC, C], side="right")]
    acc = sb("acc", [P, 2, TPC, C])
    ybt = sb("ybt", [P, KT, CH])
    zt = sb("zt", [RANK, CH])
    stats = sb("stats2", [P, TPC, 6])
    mv = sb("mv2", [P, TPC, 2])
    eps = sb("eps2", [P, 1])
    std = sb("std2", [P, TPC])
    rstd = sb("rstd2", [P, TPC])
    xn = sb("xn2", [P, TPC, C])
    xnt = sb("xnt2", [P, 2, KT, CH])
    neg = sb("neg", [P, TPC, E])
    score = sb("score", [P, TPC, E])
    biased = sb("biased", [P, TPC, E])
    above = sb("above", [P, TPC, E, E])
    equal = sb("equal", [P, TPC, E, E])
    rank = sb("rank", [P, TPC, E])
    weight = sb("weight", [P, TPC, E])
    wrest = sb("wrest", [P, TPC, E])
    wparts = sb("wparts", [P, TPC, 3, E], BF16)
    wrows = sb("wrows", [3 * E, 2, CH], BF16)
    xs = sb("xs", [P, 2, KT, CH], BF16, side="right")
    hid = sb("hid", [P, 2, NHT, CH], BF16, side="right")
    hsq = sb("hsq", [P, 2, NHT, CH], BF16, side="right")
    shid = sb("shid", [P, NHT, CH], side="right")
    shsq = sb("shsq", [P, NHT, CH], side="right")
    eout = sb("eout", [P, 2, TPC, C], BF16, side="right")
    sout = sb("sout", [P, TPC, C], side="right")

    sp_passed = sem("sp_passed2")
    dve_passed = sem("dve_passed2")
    small = sem("small")
    cast = sem("cast")
    big = sem("big")
    x_loaded = [sem("xl0"), sem("xl1")]
    y_loaded = [sem("yl0"), sem("yl1")]
    out_stored = [sem("os0"), sem("os1")]
    pre_psum = sem("pre_psum")
    pre_ready = sem("pre_ready")
    stats_done = sem("stats_done2")
    mv_ready = sem("mv_ready2")
    eps_set = sem("eps_set")
    std_ready = sem("std_ready2")
    rstd_ready = sem("rstd_ready2")
    xn_ready = sem("xn_ready2")
    route = sem("route")
    weights_split = sem("weights_split")
    wparts_ready = sem("wparts_ready")
    scale_psum = sem("scale_psum")
    xs_ready = sem("xs_ready")
    up_psum = sem("up_psum")
    hid_ready = sem("hid_ready")
    hsq_ready = sem("hsq_ready")
    down_psum = sem("down_psum")
    eout_ready = sem("eout_ready")
    added = sem("added")

    UP = [psum[:, m, :] for m in range(NHT)]
    DN = psum[:, 3:5, :]
    DNT = DN.rearrange("p b (t c) -> p (b t) c", c=C)
    SCL = psum[:, 5, :]
    PRE = psum[:, 6:8, :]
    PRET = PRE.rearrange("p b (t c) -> p (b t) c", c=C)
    PRE_STEPS = 7
    ROUTE_STEPS = 9

    def sync(sp):
        def load_y(i, p):
            n = 2 * i + p
            sp.dma_start(yb[:, p], y_all[:, bass.ds(n * TPC, TPC), :]).then_inc(y_loaded[p], 16)

        def load_x(i, p):
            n = 2 * i + p
            sp.dma_start(xb[p][:], x_ch[bass.ds(n, 1)].rearrange("o p t d -> p (o t) d")
                         ).then_inc(x_loaded[p], 16)

        def store(i, p):
            n = 2 * i + p
            wait_alone(sp, added, SLOTS * (n + 1), sp_passed)
            sp.dma_start(out_ch[bass.ds(n, 1)].rearrange("o p t d -> p (o t) d"), acc[:, p]
                         ).then_inc(out_stored[p], 16)

        def pair(i):
            for p in range(2):
                wait_alone(sp, pre_ready, PRE_STEPS * (2 * i + p) + 3, sp_passed)
                load_y(i + 1, p)
                load_x(i + 1, p)
                store(i, p)

        def ahead():
            for dst, src in ((wov, wov_t), (wou, wou_t), (gate, gate_t), (bias, bias_b), (lower, tri)):
                sp.dma_start(dst[:], src).then_inc(small, 16)

        def rest():
            sp.wait_ge(ring_used, output_placed(UNITS // B - 1))
            load_y(0, 0)
            load_x(0, 0)
            load_y(0, 1)
            sp.wait_ge(pv_done, UNITS * ST)
            load_x(0, 1)
            sp.dma_start(swup[:], swup_t).then_inc(big, 16)
            sp.dma_start(swdn[:], swdn_t).then_inc(big, 16)
            sp.wait_ge(ring_used, output_placed(UNITS - 1))
            pair(0)
            with sp.Fori(1, NCHUNK // 2 - 1) as i:
                pair(i)
            for p in range(2):
                store(NCHUNK // 2 - 1, p)
            for p in range(2):
                sp.wait_ge(out_stored[p], 16 * NCHUNK // 2)

        return ahead, rest

    def tensor(pe):
        def pre_start(n, step):
            wait_from_one(pe, pre_ready, PRE_STEPS * n + step)

        def turn_y(i, p):
            n = 2 * i + p
            pre_start(n, 0)
            pe.wait_ge(y_loaded[p], 16 * (i + 1))
            for k in range(KT):
                for t in range(TPC):
                    last = pe.transpose(PRE[:, k, t * P:(t + 1) * P], yb[:, p, t, k * P:(k + 1) * P],
                                        identf[:])
            last.then_inc(pre_psum, 1)

        def project_down(n):
            pre_start(n, 1)
            for k in range(KT):
                last = pe.matmul(PRE[0:RANK, 0, :], wov[:, k, :], ybt[:, k, :],
                                 start=k == 0, stop=k == KT - 1)
            last.then_inc(pre_psum, 1)

        def project_up(n):
            pre_start(n, 2)
            for t in range(TPC):
                last = pe.matmul(PRET[:, t, :], zt[:, t * P:(t + 1) * P], wou[:], start=True, stop=True)
            last.then_inc(pre_psum, 1)

        def turn_x(n):
            pre_start(n, 3)
            pe.wait_ge(xn_ready, n + 1)
            for k in range(KT):
                for t in range(TPC):
                    last = pe.transpose(PRE[:, k, t * P:(t + 1) * P], xn[:, t, k * P:(k + 1) * P],
                                        identf[:])
            last.then_inc(pre_psum, 1)

        def gate_logits(n, p):
            pre_start(n, 4)
            for k in range(KT):
                for t in range(TPC):
                    last = pe.matmul(PRE[t * EP:(t + 1) * EP, 0, 0:P], gate[:, k, :],
                                     xnt[:, p, k, t * P:(t + 1) * P], start=k == 0, stop=k == KT - 1)
            last.then_inc(pre_psum, 1)

        def turn_logits(n):
            pre_start(n, 5)
            pe.transpose(PRE[:, 0, 0:TPC * EP], logits[:], identf[:]).then_inc(pre_psum, 1)

        def turn_weights(n):
            pre_start(n, 6)
            pe.wait_ge(wparts_ready, n + 1)
            rows = PRE[0:3 * E, 1, :].bitcast(BF16)
            for t in range(TPC):
                last = pe.transpose(rows[:, t * P:(t + 1) * P],
                                    wparts[:, t].rearrange("p a e -> p (a e)"), identb[:])
            last.then_inc(pre_psum, 1)

        def spread(n, p, e):
            if e == 0:
                pe.wait_ge(pre_ready, PRE_STEPS * (n + 1))
            wait_from_one(pe, xs_ready, E * n + e)
            pe.matmul(SCL, pick[:, e, :], wrows[:, p, :], start=True, stop=True).then_inc(scale_psum, 1)

        def up(n, p, s, tiles=range(NHT)):
            if s < E:
                pe.wait_ge(xs_ready, E * n + s + 1)
            elif isinstance(n, int) and n == 0:
                pe.wait_ge(big, 32)
            for m in tiles:
                wait_from_one(pe, hid_ready, NHT * (SLOTS * n + s - 1) + m + 1)
                for k in range(KT):
                    cols = slice(m * P, m * P + HT[m])
                    w = wup[:, s, k, cols] if s < E else swup[:, k, cols]
                    r = xs[:, s % 2, k, :] if s < E else xnt[:, p, k, :]
                    last = pe.matmul(UP[m][0:HT[m], :], w, r, start=k == 0, stop=k == KT - 1)
                last.then_inc(up_psum, 1)

        def down(n, s):
            pe.wait_ge(hsq_ready, SLOTS * n + s + 1)
            wait_from_one(pe, eout_ready, SLOTS * n + s)
            for t in range(TPC):
                for m in range(NHT):
                    h = (hsq[0:HT[m], s % 2, m] if s < E else shsq[0:HT[m], m])[:, t * P:(t + 1) * P]
                    w = wdn[0:HT[m], s, m, :] if s < E else swdn[0:HT[m], m, :]
                    last = pe.matmul(DNT[:, t, :], h, w, start=m == 0, stop=m == NHT - 1)
            last.then_inc(down_psum, 1)

        def chunk(i, p, more=True):
            n = 2 * i + p
            ni, np_ = i + p, 1 - p
            for s in range(SLOTS):
                if more and s == 0:
                    turn_y(ni, np_)
                if s + 2 < E:
                    spread(n, p, s + 2)
                if more and s == 7:
                    up(n, p, s + 1, (0, 1))
                    turn_weights(n + 1)
                    up(n, p, s + 1, (2,))
                elif s + 1 < SLOTS:
                    up(n, p, s + 1)
                elif more:
                    up(n + 1, np_, 0)
                if more:
                    if s + 2 >= SLOTS:
                        spread(n + 1, np_, s + 2 - SLOTS)
                    if s == 0:
                        project_down(n + 1)
                    if s == 1:
                        project_up(n + 1)
                    if s == 4:
                        gate_logits(n + 1, np_)
                down(n, s)
                if more and s == 3:
                    turn_x(n + 1)
                if more and s == 4:
                    turn_logits(n + 1)

        def ahead(j):
            if j == 0:
                pe.wait_ge(small, 5 * 16)
                turn_y(0, 0)
            if j == 1:
                project_down(0)
            if j == 2:
                project_up(0)
            if j == 6:
                turn_x(0)
            if j == 8:
                gate_logits(0, 0)
            if j == 9:
                turn_logits(0)
            if j == 12:
                turn_weights(0)
            if j == ST:
                pe.wait_ge(cast, 48)
                spread(0, 0, 0)

        def rest():
            spread(0, 0, 1)
            up(0, 0, 0)
            pe.wait_ge(ring_used, output_placed(UNITS - 1))
            chunk(0, 0)
            chunk(0, 1)
            with pe.Fori(1, NCHUNK // 2 - 1) as i:
                chunk(i, 0)
                chunk(i, 1)
            chunk(NCHUNK // 2 - 1, 0)
            chunk(NCHUNK // 2 - 1, 1, more=False)

        return ahead, rest

    def scalar(act):
        def pre_copy(n, step, dst, src):
            act.wait_ge(pre_psum, PRE_STEPS * n + step + 1)
            act.activation(dst, src, ACT.Copy).then_inc(pre_ready, 1)

        def deviation(n):
            act.wait_ge(mv_ready, n + 1)
            act.activation(std[:], mv[:, :, 1], ACT.Sqrt, bias=eps[:]).then_inc(std_ready, 1)

        def gate_exp(n):
            act.wait_ge(pre_psum, PRE_STEPS * n + 6)
            wait_from_one(act, wparts_ready, n)
            turned = PRE[:, 0, 0:TPC * EP].rearrange("p (t e) -> p t e", e=EP)
            act.activation(neg[:], turned[:, :, 0:E], ACT.Exp, scale=-1.0).then_inc(pre_ready, 1)

        def relu(n, s):
            u = SLOTS * n + s
            for m in range(NHT):
                act.wait_ge(up_psum, NHT * u + m + 1)
                if m == 0:
                    wait_from_one(act, hsq_ready, u - 1)
                dst = hid[0:HT[m], s % 2, m] if s < E else shid[0:HT[m], m]
                act.activation(dst, UP[m][0:HT[m], :], ACT.Relu).then_inc(hid_ready, 1)

        def round_out(n, s):
            u = SLOTS * n + s
            act.wait_ge(down_psum, u + 1)
            wait_from_one(act, added, u - 1 if s else u)
            act.activation(eout[:, s % 2] if s < E else sout[:], DNT, ACT.Copy).then_inc(eout_ready, 1)

        def chunk(i, p, more=True):
            n = 2 * i + p
            for s in range(SLOTS):
                if more and s == 0:
                    pre_copy(n + 1, 0, ybt[:], PRE)
                if s + 1 < SLOTS:
                    relu(n, s + 1)
                elif more:
                    relu(n + 1, 0)
                if more:
                    if s == 0:
                        pre_copy(n + 1, 1, zt[:], PRE[0:RANK, 0, :])
                    if s == 2:
                        deviation(n + 1)
                    if s == 4:
                        pre_copy(n + 1, 4, logits[:], PRE[:, 0, 0:P])
                if more or s < E:
                    round_out(n, s)
                if more and s == 5:
                    gate_exp(n + 1)
                if more and s == 3:
                    pre_copy(n + 1, 3, xnt[:, 1 - p], PRE)

        def ahead(j):
            if j == 4:
                act.wait_ge(eps_set, 1)
                deviation(0)
            if j == 9:
                gate_exp(0)

        def rest():
            relu(0, 0)
            chunk(0, 0)
            chunk(0, 1)
            with act.Fori(1, NCHUNK // 2 - 1) as i:
                chunk(i, 0)
                chunk(i, 1)
            chunk(NCHUNK // 2 - 1, 0)
            chunk(NCHUNK // 2 - 1, 1, more=False)

        return ahead, rest

    def vector(dve):
        def residual(i, p):
            n = 2 * i + p
            dve.wait_ge(pre_psum, PRE_STEPS * n + 3)
            dve.wait_ge(x_loaded[p], 16 * (i + 1))
            wait_from_one(dve, out_stored[p], 16 * i)
            dve.tensor_tensor(acc[:, p], xb[p][:], PRET, ALU.add).then_inc(pre_ready, 1)

        def statistics(n, p):
            dve.wait_ge(pre_ready, PRE_STEPS * n + 3)
            for t in range(TPC):
                last = dve.bn_stats(stats[:, t, :], acc[:, p, t, :])
            last.then_inc(stats_done, 1)
            wait_alone(dve, stats_done, n + 1, dve_passed)
            for t in range(TPC):
                last = dve.bn_aggr(mv[:, t, :], stats[:, t, :])
            last.then_inc(mv_ready, 1)

        def normalise(n, p):
            dve.wait_ge(std_ready, n + 1)
            dve.reciprocal(rstd[:], std[:]).then_inc(rstd_ready, 1)
            dve.wait_ge(rstd_ready, n + 1)
            for t in range(TPC):
                last = dve.tensor_scalar(xn[:, t, :], acc[:, p, t, :], mv[:, t, 0:1],
                                         rstd[:, t:t + 1], ALU.subtract, ALU.mult)
            last.then_inc(xn_ready, 1)

        def routing(n):
            count = [ROUTE_STEPS * n]

            def then(ins):
                count[0] = count[0] + 1
                ins.then_inc(route, 1)
                dve.wait_ge(route, count[0])

            dve.wait_ge(pre_ready, PRE_STEPS * n + 6)
            then(dve.tensor_scalar(neg[:], neg[:], 1.0, None, ALU.add))
            then(dve.reciprocal(score[:], neg[:]))
            then(dve.tensor_tensor(biased[:], score[:],
                                   bias[:].unsqueeze(1).to_broadcast([P, TPC, E]), ALU.add))
            other = biased[:].unsqueeze(2).to_broadcast([P, TPC, E, E])
            own = biased[:].unsqueeze(3).to_broadcast([P, TPC, E, E])
            dve.tensor_tensor(above[:], other, own, ALU.is_gt)
            then(dve.tensor_tensor(equal[:], other, own, ALU.is_equal))
            low = lower[:].rearrange("p (a b) -> p a b", b=E).unsqueeze(1).to_broadcast([P, TPC, E, E])
            then(dve.tensor_tensor(equal[:], equal[:], low, ALU.mult))
            then(dve.tensor_tensor(above[:], above[:], equal[:], ALU.add))
            then(dve.tensor_reduce(rank[:], above[:], AX.X, ALU.add))
            then(dve.scalar_tensor_tensor(out=weight[:], in0=rank[:], scalar=2.0, in1=score[:],
                                          op0=ALU.is_lt, op1=ALU.mult))
            then(dve.tensor_copy(wparts[:, :, 0, :], weight[:]))
            assert ROUTE_STEPS == 9

        def split_weights(n):
            dve.tensor_tensor(wrest[:], weight[:], wparts[:, :, 0, :], ALU.subtract
                              ).then_inc(weights_split, 1)
            dve.wait_ge(weights_split, 2 * n + 1)
            dve.tensor_copy(wparts[:, :, 1, :], wrest[:]).then_inc(weights_split, 1)
            dve.wait_ge(weights_split, 2 * n + 2)
            dve.tensor_tensor(wparts[:, :, 2, :], wrest[:], wparts[:, :, 1, :], ALU.subtract
                              ).then_inc(wparts_ready, 1)

        def copy_weights(n, p):
            dve.wait_ge(pre_psum, PRE_STEPS * n + 7)
            dve.tensor_copy(wrows[:, p, :], PRE[0:3 * E, 1, :].bitcast(BF16)[:, 0:CH]
                            ).then_inc(pre_ready, 1)

        def scale_x(n, p, e):
            dve.wait_ge(scale_psum, E * n + e + 1)
            if e > 1:
                dve.wait_ge(up_psum, NHT * (SLOTS * n + e - 1))
            else:
                wait_from_one(dve, up_psum, NHT * (SLOTS * (n - 1) + E - 1 + e))
            dve.tensor_tensor(xs[:, e % 2], xnt[:, p], SCL.unsqueeze(1).to_broadcast([P, KT, CH]),
                              ALU.mult).then_inc(xs_ready, 1)

        def square(n, s):
            u = SLOTS * n + s
            src, dst = (hid[:, s % 2], hsq[:, s % 2]) if s < E else (shid[:], shsq[:])
            dve.wait_ge(hid_ready, NHT * (u + 1))
            wait_from_one(dve, down_psum, u - 1)
            dve.tensor_tensor(dst[:, 0:2], src[:, 0:2], src[:, 0:2], ALU.mult)
            dve.tensor_tensor(dst[0:HT[2], 2], src[0:HT[2], 2], src[0:HT[2], 2], ALU.mult
                              ).then_inc(hsq_ready, 1)

        def chunk(i, p, more=True):
            n = 2 * i + p
            ni, np_ = i + p, 1 - p
            for s in range(SLOTS):
                if more and s == 7:
                    copy_weights(n + 1, np_)
                if s + 2 < E:
                    scale_x(n, p, s + 2)
                elif more and s + 2 >= SLOTS:
                    scale_x(n + 1, np_, s + 2 - SLOTS)
                if more and s == 2:
                    statistics(n + 1, np_)
                if s + 1 < SLOTS:
                    square(n, s + 1)
                elif more:
                    square(n + 1, 0)
                if not more and s == E:
                    add_last(n, p)
                if more:
                    if s == 1:
                        residual(ni, np_)
                    if s == 2:
                        normalise(n + 1, np_)
                    if s == 5:
                        routing(n + 1)
                        split_weights(n + 1)

        def add_last(n, p):
            u = SLOTS * n + E
            dve.wait_ge(down_psum, u + 1)
            dve.wait_ge(added, u)
            dve.tensor_tensor(acc[:, p], acc[:, p], DNT, ALU.add).then_inc(added, 1)

        def copy_ahead(step, dst, src):
            dve.wait_ge(pre_psum, step + 1)
            dve.tensor_copy(dst, src).then_inc(pre_ready, 1)

        def ahead(j):
            if j == 0:
                dve.wait_ge(small, 5 * 16)
                dve.memset(eps[:], EPS).then_inc(eps_set, 1)
                copy_ahead(0, ybt[:], PRE)
            if j == 1:
                copy_ahead(1, zt[:], PRE[0:RANK, 0, :])
            if j == 2:
                residual(0, 0)
                statistics(0, 0)
            if j == 5:
                normalise(0, 0)
            if j == 6:
                copy_ahead(3, xnt[:, 0], PRE)
            if j == 8:
                copy_ahead(4, logits[:], PRE[:, 0, 0:P])
            if j == 9:
                routing(0)
                split_weights(0)
            if j == 12:
                copy_weights(0, 0)
            if j == ST:
                scale_x(0, 0, 0)

        def rest():
            scale_x(0, 0, 1)
            square(0, 0)
            chunk(0, 0)
            chunk(0, 1)
            with dve.Fori(1, NCHUNK // 2 - 1) as i:
                chunk(i, 0)
                chunk(i, 1)
            chunk(NCHUNK // 2 - 1, 0)
            chunk(NCHUNK // 2 - 1, 1, more=False)

        return ahead, rest

    def gpsimd(pool):
        def add_out(n, p, s):
            u = SLOTS * n + s
            pool.wait_ge(eout_ready, u + 1)
            wait_from_one(pool, added, u)
            pool.tensor_tensor(acc[:, p], acc[:, p], eout[:, s % 2] if s < E else sout[:], ALU.add
                               ).then_inc(added, 1)

        def chunk(i, p, more=True):
            n = 2 * i + p
            for s in range(SLOTS if more else E):
                add_out(n, p, s)

        def ahead():
            pool.wait_ge(small, 5 * 16)
            pool.dma_start(pick[:], sel).then_inc(cast, 16)
            pool.dma_start(wup[:], wup_t).then_inc(cast, 16)
            pool.dma_start(wdn[:], wdn_t).then_inc(cast, 16)

        def rest():
            chunk(0, 0)
            chunk(0, 1)
            with pool.Fori(1, NCHUNK // 2 - 1) as i:
                chunk(i, 0)
                chunk(i, 1)
            chunk(NCHUNK // 2 - 1, 0)
            chunk(NCHUNK // 2 - 1, 1, more=False)

        return ahead, rest

    return {"sync": sync, "tensor": tensor, "scalar": scalar, "vector": vector, "gpsimd": gpsimd}


def kernel(**inputs):
    import numpy as np
    import concourse.bacc as bacc
    from concourse.bass_utils import run_bass_kernel_spmd

    def a(name):
        return np.asarray(inputs[name])

    def by_partition(w):
        k, n = w.shape
        tiles = -(-k // P)
        full = np.zeros((tiles * P, n), w.dtype)
        full[:k] = w
        return full.reshape(tiles, P, n).transpose(1, 0, 2)

    gate_columns = np.zeros((C, EP), a("L0_ffn_gate_w").dtype)
    gate_columns[:, 0:E] = a("L0_ffn_gate_w").T
    experts = range(E)
    eye3 = np.zeros((3, E, E, P), np.float32)
    for e in experts:
        eye3[:, e, e, :] = 1.0
    arrays = {
        "x": a("L0_attn_x"),
        "wv_t": by_partition(a("L0_attn_W_qkv_v").T),
        "wu_t": a("L0_attn_W_qkv_u").T,
        "wov_t": by_partition(a("L0_attn_W_o_v").T),
        "wou_t": a("L0_attn_W_o_u").T,
        "gate_t": by_partition(gate_columns),
        "bias_b": np.tile(a("L0_ffn_expert_bias")[None, :], (P, 1)),
        "wup_t": np.stack([by_partition(a("L0_ffn_w_up")[e].T) for e in experts], 1),
        "wdn_t": np.stack([by_partition(a("L0_ffn_w_down")[e].T) for e in experts], 1),
        "swup_t": by_partition(a("L0_ffn_shared_w_up").T),
        "swdn_t": by_partition(a("L0_ffn_shared_w_down").T),
        "ident": np.eye(P, dtype=np.float32),
        "tri": np.tile(np.tril(np.ones((E, E), np.float32), -1).reshape(1, E * E), (P, 1)),
        "sel": eye3.reshape(3 * E, E, P),
    }
    arrays = {k: np.ascontiguousarray(v) for k, v in arrays.items()}
    nc = bacc.Bacc("TRN2", target_bir_lowering=False, num_devices=1)
    args = [nc.dram_tensor(k, v.shape, mybir.dt.from_np(v.dtype), kind="ExternalInput").ap()
            for k, v in arrays.items()]
    args.append(nc.dram_tensor("out", (B, T, C), F32, kind="ExternalOutput").ap())
    build(nc, *args)
    r = run_bass_kernel_spmd(nc, [arrays], core_ids=[0])
    return r.results[0]["out"]
```
